# Optimizing a Trainium2 kernel written in Bass

```python
import numpy as np
import jax
import jax.numpy as jnp

def _softmax(x, axis=-1):
    return jax.nn.softmax(x, axis=axis)

def _gelu(x):
    return jax.nn.gelu(x, approximate=True)

def _silu(x):
    return jax.nn.silu(x)

def _sigmoid(x):
    return jax.nn.sigmoid(x)

def _layernorm(x, axis=-1, eps=1e-05):
    m = jnp.mean(x, axis=axis, keepdims=True)
    v = jnp.var(x, axis=axis, keepdims=True)
    return (x - m) / jnp.sqrt(v + eps)

def _scatter_add(tgt, idx, src, axis=0):
    return tgt.at[idx].add(src)

def _segment_sum(src, seg, n):
    return jax.ops.segment_sum(src, seg, n)
kernel_name = 'mk_gnn_resnorm_d4_gnn_r8_3928dd'

def setup_inputs(seed: int=0):
    np.random.seed(seed)
    _w = jnp.asarray

    def _rec_inputs():
        import jax
        import jax.numpy as jnp
        _gk = jax.random.key(seed)
        x = -0.000202 + 1 * jax.random.normal(jax.random.fold_in(_gk, 1), (6250, 128), jnp.float32)
        _s = jax.random.randint(jax.random.fold_in(_gk, 2), (50000,), 0, 6250, jnp.int32)
        _d = jax.random.randint(jax.random.fold_in(_gk, 3), (50000,), 0, 6250, jnp.int32)
        _loop = jnp.arange(6250, dtype=jnp.int32)
        src = jnp.concatenate([_s, _d, _loop])
        dst = jnp.concatenate([_d, _s, _loop])
        _o = jnp.argsort(dst, stable=True)
        src = src[_o]
        dst = dst[_o]
        edge_attr_64 = -0.000128692 + 0.999872 * jax.random.normal(jax.random.fold_in(_gk, 11), (106250, 64), jnp.float32)
        edge_type_16 = jax.random.randint(jax.random.fold_in(_gk, 13), (106250,), 0, 16, jnp.int32)
        edge_weight = jax.random.uniform(jax.random.fold_in(_gk, 14), (106250,), jnp.float32, 0.0, 0.999998)
        return (x, src, dst, edge_attr_64, edge_type_16, edge_weight)
    x, src, dst, edge_attr_64, edge_type_16, edge_weight = _rec_inputs()

    def _L0_gnn_setup():
        import jax, jax.numpy as jnp
        import numpy as np
        N, E, H, EC, K, NH = (6250, 80000, 128, 64, 128, 4)
        Hh, Kh = (H // NH, K // NH)
        LOG2 = float(np.log(2.0))

        def ssp(x):
            return jax.nn.softplus(x) - LOG2

        def ln(x, g, b, eps=1e-05):
            m = jnp.mean(x, axis=-1, keepdims=True)
            v = jnp.var(x, axis=-1, keepdims=True)
            return (x - m) * jax.lax.rsqrt(v + eps) * g + b
        key = jax.random.key(seed)
        ks = jax.random.split(key, 24)

        def nrm(k, shape, scale):
            return jax.random.normal(k, shape, jnp.float32) * scale
        s_h = 1.0 / np.sqrt(Hh)
        s_e = 1.0 / np.sqrt(EC)
        s_k = 1.0 / np.sqrt(Kh)
        inp = {}
        inp['x'] = nrm(ks[0], (N, H), 1.0)
        inp['edge_attr'] = nrm(ks[1], (E, EC), 1.0)
        inp['edge_index'] = jax.random.randint(ks[2], (2, E), 0, N)
        inp['k_w'] = nrm(ks[3], (NH, Kh, Hh), s_h)
        inp['q_w'] = nrm(ks[4], (NH, Kh, Hh), s_h)
        inp['v_w'] = nrm(ks[5], (NH, Hh, Hh), s_h)
        inp['wk1_w'] = nrm(ks[6], (Kh, EC), s_e)
        inp['wk1_b'] = nrm(ks[7], (Kh,), 0.01)
        inp['wk2_w'] = nrm(ks[8], (Kh, Kh), s_k)
        inp['wk2_b'] = nrm(ks[9], (Kh,), 0.01)
        inp['wkl_w'] = nrm(ks[10], (Kh, Kh), s_k)
        inp['wkl_b'] = nrm(ks[11], (Kh,), 0.01)
        inp['wv1_w'] = nrm(ks[12], (Hh, EC), s_e)
        inp['wv1_b'] = nrm(ks[13], (Hh,), 0.01)
        inp['wv2_w'] = nrm(ks[14], (Hh, Hh), s_h)
        inp['wv2_b'] = nrm(ks[15], (Hh,), 0.01)
        inp['wvl_w'] = nrm(ks[16], (Hh, Hh), s_h)
        inp['wvl_b'] = nrm(ks[17], (Hh,), 0.01)
        inp['out_w'] = nrm(ks[18], (H, H), 1.0 / np.sqrt(H))
        inp['out_b'] = nrm(ks[19], (H,), 0.01)
        inp['ln1_g'] = jnp.ones((H,), jnp.float32)
        inp['ln1_b'] = jnp.zeros((H,), jnp.float32)
        inp['ln2_g'] = jnp.ones((H,), jnp.float32)
        inp['ln2_b'] = jnp.zeros((H,), jnp.float32)
        return inp
    _L0_gnn_all = _L0_gnn_setup()
    _L0_gnn_in = {k: v for k, v in _L0_gnn_all.items() if k in ('k_w', 'q_w', 'v_w', 'wk1_w', 'wk1_b', 'wk2_w', 'wk2_b', 'wkl_w', 'wkl_b', 'wv1_w', 'wv1_b', 'wv2_w', 'wv2_b', 'wvl_w', 'wvl_b', 'out_w', 'out_b', 'ln1_g', 'ln1_b', 'ln2_g', 'ln2_b')}
    del _L0_gnn_all

    def _L1_gnn_setup():
        import jax, jax.numpy as jnp
        import numpy as np
        N, E, D = (12500, 200000, 128)
        key = jax.random.key(seed)
        ks = jax.random.split(key, 10)
        inp = {'x': jax.random.normal(ks[0], (N, D), dtype=jnp.float32), 'edge_index': jax.random.randint(ks[1], (2, E), 0, N, dtype=jnp.int64), 'Wp': jax.random.normal(ks[2], (D, D), dtype=jnp.float32) * 0.05, 'bp': jnp.zeros((D,), dtype=jnp.float32), 'W0': jax.random.normal(ks[3], (D, D), dtype=jnp.float32) * 0.05, 'b0': jnp.zeros((D,), dtype=jnp.float32), 'W1': jax.random.normal(ks[4], (D, D), dtype=jnp.float32) * 0.05, 'b1': jnp.zeros((D,), dtype=jnp.float32), 'W2': jax.random.normal(ks[5], (D, D), dtype=jnp.float32) * 0.05, 'b2': jnp.zeros((D,), dtype=jnp.float32)}
        return inp
    _L1_gnn_all = _L1_gnn_setup()
    _L1_gnn_in = {k: v for k, v in _L1_gnn_all.items() if k in ('Wp', 'bp', 'W0', 'b0', 'W1', 'b1', 'W2', 'b2')}
    del _L1_gnn_all

    def _L2_gnn_setup():
        import jax, jax.numpy as jnp
        import numpy as np
        N = 12500
        D = 128
        E = 75000
        key = jax.random.key(seed)
        k = jax.random.split(key, 7)
        x = jax.random.normal(k[0], (N, D), dtype=jnp.float32)
        edge_index = jax.random.randint(k[1], (2, E), 0, N, dtype=jnp.int32)
        edge_weight = jax.random.uniform(k[2], (E,), dtype=jnp.float32)
        s = 1.0 / np.sqrt(D)
        W1 = jax.random.uniform(k[3], (D, D), minval=-s, maxval=s, dtype=jnp.float32)
        b1 = jax.random.uniform(k[4], (D,), minval=-s, maxval=s, dtype=jnp.float32)
        W2 = jax.random.uniform(k[5], (D, D), minval=-s, maxval=s, dtype=jnp.float32)
        b2 = jax.random.uniform(k[6], (D,), minval=-s, maxval=s, dtype=jnp.float32)
        return {'x': x, 'edge_index': edge_index, 'edge_weight': edge_weight, 'W1': W1, 'b1': b1, 'W2': W2, 'b2': b2}
    _L2_gnn_all = _L2_gnn_setup()
    _L2_gnn_in = {k: v for k, v in _L2_gnn_all.items() if k in ('W1', 'b1', 'W2', 'b2')}
    del _L2_gnn_all

    def _L3_gnn_setup():
        import jax, jax.numpy as jnp
        import numpy as np
        N, E = (6250, 200000)
        IN_F, OUT_F = (128, 128)
        T, B = (16, 8)
        LN_EPS = 1e-05
        key = jax.random.key(seed)
        ks = jax.random.split(key, 6)
        x = jax.random.normal(ks[0], (N, IN_F), dtype=jnp.float32)
        edge_index = jax.random.randint(ks[1], (2, E), 0, N, dtype=jnp.int64)
        edge_type = jax.random.randint(ks[2], (E,), 0, T, dtype=jnp.int64)
        edge_weight = jnp.ones((E,), dtype=jnp.float32)
        weight = jax.random.normal(ks[3], (B, IN_F, OUT_F), dtype=jnp.float32) * 0.05
        alpha = jax.random.normal(ks[4], (T, B), dtype=jnp.float32) * 0.05
        bias = jnp.zeros((OUT_F,), dtype=jnp.float32)
        w_self = jax.random.normal(ks[5], (IN_F, OUT_F), dtype=jnp.float32) * 0.05
        ln_gamma = jnp.ones((OUT_F,), dtype=jnp.float32)
        ln_beta = jnp.zeros((OUT_F,), dtype=jnp.float32)
        return {'x': x, 'edge_index': edge_index, 'edge_type': edge_type, 'edge_weight': edge_weight, 'weight': weight, 'alpha': alpha, 'bias': bias, 'w_self': w_self, 'ln_gamma': ln_gamma, 'ln_beta': ln_beta}
    _L3_gnn_all = _L3_gnn_setup()
    _L3_gnn_in = {k: v for k, v in _L3_gnn_all.items() if k in ('weight', 'alpha', 'bias', 'w_self', 'ln_gamma', 'ln_beta')}
    del _L3_gnn_all
    return {'x': x, 'src': src, 'dst': dst, 'edge_attr_64': edge_attr_64, 'edge_type_16': edge_type_16, 'edge_weight': edge_weight, 'L0_gnn_k_w': _L0_gnn_in['k_w'], 'L0_gnn_q_w': _L0_gnn_in['q_w'], 'L0_gnn_v_w': _L0_gnn_in['v_w'], 'L0_gnn_wk1_w': _L0_gnn_in['wk1_w'], 'L0_gnn_wk1_b': _L0_gnn_in['wk1_b'], 'L0_gnn_wk2_w': _L0_gnn_in['wk2_w'], 'L0_gnn_wk2_b': _L0_gnn_in['wk2_b'], 'L0_gnn_wkl_w': _L0_gnn_in['wkl_w'], 'L0_gnn_wkl_b': _L0_gnn_in['wkl_b'], 'L0_gnn_wv1_w': _L0_gnn_in['wv1_w'], 'L0_gnn_wv1_b': _L0_gnn_in['wv1_b'], 'L0_gnn_wv2_w': _L0_gnn_in['wv2_w'], 'L0_gnn_wv2_b': _L0_gnn_in['wv2_b'], 'L0_gnn_wvl_w': _L0_gnn_in['wvl_w'], 'L0_gnn_wvl_b': _L0_gnn_in['wvl_b'], 'L0_gnn_out_w': _L0_gnn_in['out_w'], 'L0_gnn_out_b': _L0_gnn_in['out_b'], 'L0_gnn_ln1_g': _L0_gnn_in['ln1_g'], 'L0_gnn_ln1_b': _L0_gnn_in['ln1_b'], 'L0_gnn_ln2_g': _L0_gnn_in['ln2_g'], 'L0_gnn_ln2_b': _L0_gnn_in['ln2_b'], 'L1_gnn_Wp': _L1_gnn_in['Wp'], 'L1_gnn_bp': _L1_gnn_in['bp'], 'L1_gnn_W0': _L1_gnn_in['W0'], 'L1_gnn_b0': _L1_gnn_in['b0'], 'L1_gnn_W1': _L1_gnn_in['W1'], 'L1_gnn_b1': _L1_gnn_in['b1'], 'L1_gnn_W2': _L1_gnn_in['W2'], 'L1_gnn_b2': _L1_gnn_in['b2'], 'L2_gnn_W1': _L2_gnn_in['W1'], 'L2_gnn_b1': _L2_gnn_in['b1'], 'L2_gnn_W2': _L2_gnn_in['W2'], 'L2_gnn_b2': _L2_gnn_in['b2'], 'L3_gnn_weight': _L3_gnn_in['weight'], 'L3_gnn_alpha': _L3_gnn_in['alpha'], 'L3_gnn_bias': _L3_gnn_in['bias'], 'L3_gnn_w_self': _L3_gnn_in['w_self'], 'L3_gnn_ln_gamma': _L3_gnn_in['ln_gamma'], 'L3_gnn_ln_beta': _L3_gnn_in['ln_beta']}

def reference(x, src, dst, edge_attr_64, edge_type_16, edge_weight, L0_gnn_k_w, L0_gnn_q_w, L0_gnn_v_w, L0_gnn_wk1_w, L0_gnn_wk1_b, L0_gnn_wk2_w, L0_gnn_wk2_b, L0_gnn_wkl_w, L0_gnn_wkl_b, L0_gnn_wv1_w, L0_gnn_wv1_b, L0_gnn_wv2_w, L0_gnn_wv2_b, L0_gnn_wvl_w, L0_gnn_wvl_b, L0_gnn_out_w, L0_gnn_out_b, L0_gnn_ln1_g, L0_gnn_ln1_b, L0_gnn_ln2_g, L0_gnn_ln2_b, L1_gnn_Wp, L1_gnn_bp, L1_gnn_W0, L1_gnn_b0, L1_gnn_W1, L1_gnn_b1, L1_gnn_W2, L1_gnn_b2, L2_gnn_W1, L2_gnn_b1, L2_gnn_W2, L2_gnn_b2, L3_gnn_weight, L3_gnn_alpha, L3_gnn_bias, L3_gnn_w_self, L3_gnn_ln_gamma, L3_gnn_ln_beta):
    import jax
    import jax.numpy as jnp

    def _L0_gnn_ref(x, edge_attr, k_w, q_w, v_w, wk1_w, wk1_b, wk2_w, wk2_b, wkl_w, wkl_b, wv1_w, wv1_b, wv2_w, wv2_b, wvl_w, wvl_b, out_w, out_b, ln1_g, ln1_b, ln2_g, ln2_b, edge_index):
        import jax, jax.numpy as jnp
        import numpy as np
        N, E, H, EC, K, NH = (6250, 80000, 128, 64, 128, 4)
        Hh, Kh = (H // NH, K // NH)
        LOG2 = float(np.log(2.0))

        def ssp(x):
            return jax.nn.softplus(x) - LOG2

        def ln(x, g, b, eps=1e-05):
            m = jnp.mean(x, axis=-1, keepdims=True)
            v = jnp.var(x, axis=-1, keepdims=True)
            return (x - m) * jax.lax.rsqrt(v + eps) * g + b
        row, col = (edge_index[0], edge_index[1])
        y = ln(x, ln1_g, ln1_b)
        yh = y.reshape(N, NH, Hh)
        h_k = jnp.einsum('nhd,hkd->nhk', yh, k_w)
        h_q = jnp.einsum('nhd,hkd->nhk', yh, q_w)
        h_v = jnp.einsum('nhd,hkd->nhk', yh, v_w)
        Wk = ssp(edge_attr @ wk1_w.T + wk1_b) @ wk2_w.T + wk2_b
        keys_j = jnp.einsum('ehk,jk->ehj', Wk[:, None, :] * h_k[col], wkl_w) + wkl_b
        qk = jnp.sum(h_q[row] * keys_j, axis=-1)
        m = jax.ops.segment_max(qk, row, num_segments=N)
        ex = jnp.exp(qk - m[row])
        denom = jax.ops.segment_sum(ex, row, num_segments=N)
        alpha = ex / denom[row]
        Wv = ssp(edge_attr @ wv1_w.T + wv1_b) @ wv2_w.T + wv2_b
        msg = jnp.einsum('ehd,jd->ehj', Wv[:, None, :] * h_v[col], wvl_w) + wvl_b
        msg = alpha[..., None] * msg
        aggr = jax.ops.segment_sum(msg, row, num_segments=N).reshape(N, H)
        x2 = aggr + x
        y2 = ln(x2, ln2_g, ln2_b)
        return ssp(y2) @ out_w.T + out_b + x2

    def _L1_gnn_ref(x, edge_index, Wp, bp, W0, b0, W1, b1, W2, b2):
        import jax, jax.numpy as jnp
        import numpy as np
        N, E, D = (12500, 200000, 128)
        n = x.shape[0]
        h = jax.nn.gelu(x @ Wp + bp, approximate=False)
        loops = jnp.arange(n)
        src = jnp.concatenate([edge_index[0], loops])
        dst = jnp.concatenate([edge_index[1], loops])
        deg = jax.ops.segment_sum(jnp.ones(src.shape[0], h.dtype), dst, num_segments=n)
        dinv = jnp.where(deg > 0, jax.lax.rsqrt(deg), 0.0)
        norm = dinv[src] * dinv[dst]
        for W, b in ((W0, b0), (W1, b1), (W2, b2)):
            msg = (h @ W)[src] * norm[:, None]
            h = jax.ops.segment_sum(msg, dst, num_segments=n) + b
        return h

    def _L2_gnn_ref(x, edge_index, edge_weight, W1, b1, W2, b2):
        import jax, jax.numpy as jnp
        import numpy as np
        N = 12500
        D = 128
        E = 75000
        row, col = (edge_index[0], edge_index[1])
        msgs = edge_weight[:, None] * x[row]
        agg = jax.ops.segment_sum(msgs, col, num_segments=x.shape[0])
        h = (agg + x) @ W1.T + b1 + agg * x @ W2.T + b2
        out = jax.nn.leaky_relu(h, negative_slope=0.2)
        return out

    def _L3_gnn_ref(x, edge_index, edge_type, edge_weight, weight, alpha, bias, w_self, ln_gamma, ln_beta):
        import jax, jax.numpy as jnp
        import numpy as np
        N, E = (6250, 200000)
        IN_F, OUT_F = (128, 128)
        T, B = (16, 8)
        LN_EPS = 1e-05
        n = x.shape[0]
        row, col = (edge_index[0], edge_index[1])
        deg = jax.ops.segment_sum(edge_weight, row, num_segments=n)
        norm_w = edge_weight / jnp.maximum(deg[row], 1e-12)
        W = jnp.einsum('tb,bio->tio', alpha, weight)
        h_all = jnp.einsum('ni,tio->tno', x, W)
        msgs = h_all[edge_type, col] * norm_w[:, None]
        h = jax.ops.segment_sum(msgs, row, num_segments=n)
        mu = jnp.mean(h, axis=-1, keepdims=True)
        var = jnp.mean((h - mu) ** 2, axis=-1, keepdims=True)
        h = (h - mu) * jax.lax.rsqrt(var + LN_EPS) * ln_gamma + ln_beta
        h = h + bias
        h = h + x @ w_self
        return h
    edge_index = jnp.stack([src, dst])
    x = _layernorm(x + _L0_gnn_ref(x, edge_attr_64, L0_gnn_k_w, L0_gnn_q_w, L0_gnn_v_w, L0_gnn_wk1_w, L0_gnn_wk1_b, L0_gnn_wk2_w, L0_gnn_wk2_b, L0_gnn_wkl_w, L0_gnn_wkl_b, L0_gnn_wv1_w, L0_gnn_wv1_b, L0_gnn_wv2_w, L0_gnn_wv2_b, L0_gnn_wvl_w, L0_gnn_wvl_b, L0_gnn_out_w, L0_gnn_out_b, L0_gnn_ln1_g, L0_gnn_ln1_b, L0_gnn_ln2_g, L0_gnn_ln2_b, edge_index), axis=-1)
    x = _layernorm(x + _L1_gnn_ref(x, edge_index, L1_gnn_Wp, L1_gnn_bp, L1_gnn_W0, L1_gnn_b0, L1_gnn_W1, L1_gnn_b1, L1_gnn_W2, L1_gnn_b2), axis=-1)
    x = _layernorm(x + _L2_gnn_ref(x, edge_index, edge_weight, L2_gnn_W1, L2_gnn_b1, L2_gnn_W2, L2_gnn_b2), axis=-1)
    x = _layernorm(x + _L3_gnn_ref(x, edge_index, edge_type_16, edge_weight, L3_gnn_weight, L3_gnn_alpha, L3_gnn_bias, L3_gnn_w_self, L3_gnn_ln_gamma, L3_gnn_ln_beta), axis=-1)
    return x

_drawn_inputs = setup_inputs


def setup_inputs(seed=0):
    import zlib

    import numpy as np

    out = dict(_drawn_inputs(seed))
    spreads = {'L0_gnn_ln1_g': (1.0, 0.2),
     'L0_gnn_ln1_b': (0.0, 0.1),
     'L0_gnn_ln2_g': (1.0, 0.2),
     'L0_gnn_ln2_b': (0.0, 0.1),
     'L1_gnn_bp': (0.0, 0.304),
     'L1_gnn_b0': (0.0, 0.1),
     'L1_gnn_b1': (0.0, 0.1),
     'L1_gnn_b2': (0.0, 0.1),
     'L3_gnn_bias': (0.0, 0.1),
     'L3_gnn_ln_gamma': (1.0, 0.2),
     'L3_gnn_ln_beta': (0.0, 0.1)}
    factors = {'L0_gnn_wk1_b': 8.0,
     'L0_gnn_wk2_b': 7.572,
     'L0_gnn_wkl_b': 64.0,
     'L0_gnn_wv1_b': 22.486,
     'L0_gnn_wv2_b': 8.0,
     'L0_gnn_wvl_b': 4.493,
     'L0_gnn_out_b': 4.37,
     'L1_gnn_Wp': 4.065,
     'L2_gnn_b1': 2.882,
     'L2_gnn_b2': 2.802}
    for name, (base, spread) in spreads.items():
        noise = np.random.default_rng([zlib.crc32(name.encode()), seed]).standard_normal(out[name].shape)
        drawn = base * np.exp(spread * noise) if base else spread * noise
        out[name] = jnp.asarray(drawn.astype(out[name].dtype))
    for name, factor in factors.items():
        out[name] = (out[name] * factor).astype(out[name].dtype)
    return out
```

```python
from contextlib import ExitStack

import numpy as np
import concourse.bass as bass
from concourse import mybir

F32 = mybir.dt.float32
I32 = mybir.dt.int32
U32 = mybir.dt.uint32
ALU = mybir.AluOpType
ACT = mybir.ActivationFunctionType
AX = mybir.AxisListType.X

P = 128
LN_EPS = 1e-5
BIG = 3.0e38
HALF = 4
SLOTS = 2 * HALF
TABLES = 4
MTABLES = 8
GB = 5


class Sem:

    def __init__(self, handle):
        self.h = handle
        self.base = 0

    def at(self, v):
        return self.base + v

    def past(self, v):
        self.base += v


def build(nc, I, out):
    N, D = I["x"].shape
    E, EC = I["edge_attr_64"].shape
    NH, KH, _ = I["L0_gnn_k_w"].shape
    NT, NBAS = I["L3_gnn_alpha"].shape
    PU = 125
    NB = N // PU
    assert PU * NB == N and NB % GB == 0
    NP = P * NB
    assert N + P <= NP
    STRIDE = (E // P // 10) * 10
    T = E - (P - 1) * STRIDE
    assert STRIDE <= T and T % SLOTS == 0
    OVER = T - STRIDE
    ITERS = T // SLOTS
    TI = T + HALF
    LOG2 = float(np.log(2.0))
    QW = D + NH

    top = ExitStack()
    names = [0]
    n_loads = []

    def sb(ctx, name, shape, dt=F32):
        names[0] += 1
        return ctx.enter_context(nc.sbuf_tensor(f"{name}_{names[0]}", shape, dt))

    def ps(ctx, name, shape, dt=F32):
        names[0] += 1
        return ctx.enter_context(nc.psum_tensor(f"{name}_{names[0]}", shape, dt))

    def sem(name):
        return Sem(top.enter_context(nc.semaphore(name)))

    def dram(name, shape):
        return nc.dram_tensor(name, shape, F32, kind="Internal").ap()

    def linker(eng, s):
        def link(ins):
            s.past(1)
            ins.then_inc(s.h, 1)
            eng.wait_ge(s.h, s.base)
        return link

    kv_t = dram("kv_t", (NP, 2 * D))
    q_t = dram("q_t", (NP, QW))
    m_t = dram("m_t", (NP, NH))
    h_t = dram("h_t", (NP, D))
    rel_t = dram("rel_t", (NP * NT, D))
    u_d = dram("u_d", (P, T * D))
    mx = [dram(f"mx{k}", (NP, NH)) for k in range(MTABLES)]
    acc_n = [dram(f"accn{k}", (NP, QW)) for k in range(TABLES)]
    acc = [[dram(f"acc{j}_{k}", (NP, D)) for k in range(TABLES)] for j in range(5)]

    with top:
        s_v = sem("dve_chain")
        s_a = sem("act_chain")
        s_p = sem("pool_chain")
        s_t = sem("pe_chain")
        s_ld = sem("loads_landed")
        s_st = sem("stores_landed")
        s_x1 = sem("stage_signal_1")
        s_x2 = sem("stage_signal_2")
        s_x3 = sem("stage_signal_3")
        s_x4 = sem("stage_signal_4")

        def consts(c):
            return sb(top, *c)

        srcf = sb(top, "srcf", [P, TI])
        dstf = sb(top, "dstf", [P, TI])
        wf = sb(top, "wf", [P, TI])
        src_i = sb(top, "src_i", [P, TI], I32)
        dst_i = sb(top, "dst_i", [P, TI], I32)
        ssc_i = sb(top, "ssc_i", [P, TI], I32)
        dsc_i = sb(top, "dsc_i", [P, TI], I32)
        rel_i = sb(top, "rel_i", [P, TI], I32)
        ident = sb(top, "ident", [P, P])
        ones = sb(top, "ones", [P, P])
        trash = sb(top, "trash", [P, 1])
        epsc = sb(top, "epsc", [P, 1])
        halfc = sb(top, "halfc", [P, 1])
        X = sb(top, "X", [P, NB, D])
        Y = sb(top, "Y", [P, NB, D])
        Z = sb(top, "Z", [P, NB, D])
        V = sb(top, "V", [P, NB, D])
        degd = sb(top, "degd", [P, NB])
        degs = sb(top, "degs", [P, NB])
        dinv = sb(top, "dinv", [P, NB])
        red = sb(top, "red", [P, NB])
        red2 = sb(top, "red2", [P, NB])
        rowb = sb(top, "rowb", [P, 4, D])

        def bc_mid(ap2, n):
            return ap2.unsqueeze(1).to_broadcast([ap2.shape[0], n, ap2.shape[1]])

        def bc_last(ap2, n):
            return ap2.unsqueeze(2).to_broadcast([ap2.shape[0], ap2.shape[1], n])

        def over(ap1, width):
            return bass.AP(ap1.tensor, 0, [[STRIDE * width, P], [1, T * width]])

        with ExitStack() as c:
            isrc = sb(c, "isrc", [P, T], I32)
            idst = sb(c, "idst", [P, T], I32)
            ityp = sb(c, "ityp", [P, T], I32)
            last = sb(c, "last", [P, 1])
            nlast = sb(c, "nlast", [P, 1])
            ptmp = sb(c, "ptmp", [P, 1])
            tf = sb(c, "tf", [P, TI])
            block = c.enter_context(nc.Block())

            @block.sync
            def _(sp):
                sp.dma_start(isrc[:, :], over(I["src"], 1)).then_inc(s_ld.h, 16)
                sp.dma_start(idst[:, :], over(I["dst"], 1)).then_inc(s_ld.h, 16)
                sp.dma_start(ityp[:, :], over(I["edge_type_16"], 1)).then_inc(s_ld.h, 16)
                sp.dma_start(wf[:, 0:T], over(I["edge_weight"], 1)).then_inc(s_ld.h, 16)
                sp.wait_ge(s_x1.h, 1)
                sp.dma_start(X[0:PU, :, :], I["x"].rearrange("(p b) d -> p b d", b=NB)).then_inc(s_ld.h, 16)
                sp.wait_ge(s_ld.h, 80)

            @block.gpsimd
            def _(pool):
                link = linker(pool, s_p)
                link(nc.gpsimd.memset(ident[:, :], 0.0))
                link(nc.gpsimd.affine_select(out=ident[:, :], in_=ident[:, :], compare_op=ALU.not_equal, fill=1.0,
                                             base=0, pattern=[[-1, P]], channel_multiplier=1))
                link(nc.gpsimd.iota(trash[:, :], [[0, 1]], base=N, channel_multiplier=1,
                                    allow_small_or_imprecise_dtypes=True))

            @block.vector
            def _(dve):
                link = linker(dve, s_v)
                dve.memset(ones[:, :], 1.0)
                dve.memset(epsc[:, :], LN_EPS)
                dve.memset(halfc[:, :], 0.5)
                dve.memset(wf[:, T:TI], 0.0)
                dve.memset(X[:, :, :], 0.0).then_inc(s_x1.h, 1)
                dve.wait_ge(s_ld.h, 80)
                dve.wait_ge(s_p.h, 3)
                link(dve.tensor_scalar(last[:, :], trash[:, :], float(N + P - 1), None, ALU.is_equal))
                link(dve.tensor_scalar(nlast[:, :], last[:, :], -float(N), float(N), ALU.mult, ALU.add))
                for raw, keyf, key_i in ((isrc, srcf, src_i), (idst, dstf, dst_i)):
                    link(dve.tensor_copy(keyf[:, 0:T], raw[:, :]))
                    link(dve.tensor_scalar(keyf[:, STRIDE:T], keyf[:, STRIDE:T], last[:, 0:1], nlast[:, 0:1],
                                           ALU.mult, ALU.add))
                    link(dve.memset(keyf[:, T:TI], float(N)))
                    link(dve.tensor_copy(key_i[:, :], keyf[:, :]))
                link(dve.tensor_scalar(wf[:, STRIDE:T], wf[:, STRIDE:T], last[:, 0:1], None, ALU.mult))
                link(dve.memset(tf[:, :], 0.0))
                link(dve.tensor_copy(tf[:, 0:T], ityp[:, :]))
                link(dve.scalar_tensor_tensor(tf[:, :], dstf[:, :], float(NT), tf[:, :], ALU.mult, ALU.add))
                link(dve.tensor_copy(rel_i[:, :], tf[:, :]))

            s_ld.past(80)
            s_x1.past(1)

        def index_stage(keyf, scat_i, deg, weighted, n_bc, n_eq):
            with ExitStack() as c:
                tri = sb(c, "tri", [P, P])
                ioh = sb(c, "ioh", [P, P])
                hi = sb(c, "hi", [P, TI])
                lo = sb(c, "lo", [P, TI])
                ti = sb(c, "ti", [P, TI], I32)
                tf = sb(c, "tf", [P, TI])
                before = sb(c, "before", [P, T])
                diag = sb(c, "diag", [P, 2, HALF, P])
                junk = sb(c, "junk", [P, 2, HALF, P])
                ohh = sb(c, "ohh", [P, 2, HALF, P])
                ohl = sb(c, "ohl", [P, 2, HALF, NB])
                zero = sb(c, "zero", [P, P])
                pbc = ps(c, "pbc", [P, 2, HALF, P])
                pdeg = ps(c, "pdeg", [P, 512])
                block = c.enter_context(nc.Block())
                s_d, s_b, s_f, s_o, s_q = n_bc, n_eq, s_x1, s_x2, s_x3

                @block.gpsimd
                def _(pool):
                    link = linker(pool, s_p)
                    link(nc.gpsimd.memset(tri[:, :], 1.0))
                    link(nc.gpsimd.affine_select(out=tri[:, :], in_=tri[:, :], compare_op=ALU.is_gt, fill=0.0,
                                                 base=0, pattern=[[-1, P]], channel_multiplier=1))
                    nc.gpsimd.iota(ioh[:, :], [[1, P]], base=0, channel_multiplier=0,
                                   allow_small_or_imprecise_dtypes=True).then_inc(s_x4.h, 1)

                @block.vector
                def _(dve):
                    link = linker(dve, s_v)
                    dve.memset(zero[:, :], 0.0).then_inc(s_x4.h, 1)
                    dve.wait_ge(s_x4.h, s_x4.at(2))
                    link(dve.tensor_scalar(tf[:, :], keyf[:, :], 1.0 / NB, None, ALU.mult))
                    link(dve.tensor_copy(ti[:, :], tf[:, :]))
                    link(dve.tensor_copy(hi[:, :], ti[:, :]))
                    link(dve.scalar_tensor_tensor(lo[:, :], hi[:, :], -float(NB), keyf[:, :], ALU.mult, ALU.add))
                    link(dve.tensor_scalar(tf[:, :], lo[:, :], 0.0, None, ALU.is_lt))
                    link(dve.tensor_tensor(hi[:, :], hi[:, :], tf[:, :], ALU.subtract))
                    link(dve.scalar_tensor_tensor(lo[:, :], tf[:, :], float(NB), lo[:, :], ALU.mult, ALU.add))
                    link(dve.tensor_scalar(tf[:, :], lo[:, :], float(NB), None, ALU.is_ge))
                    link(dve.tensor_tensor(hi[:, :], hi[:, :], tf[:, :], ALU.add))
                    link(dve.scalar_tensor_tensor(lo[:, :], tf[:, :], -float(NB), lo[:, :], ALU.mult, ALU.add))
                    with dve.Fori(0, ITERS) as i:
                        for h in range(2):
                            c0 = i * SLOTS + h * HALF
                            dve.wait_ge(s_b.h, s_b.at(i * 2))
                            dve.tensor_tensor(diag[:, h, :, :], bc_mid(ident[:, :], HALF),
                                              bc_last(keyf[:, bass.ds(c0, HALF)], P), ALU.mult).then_inc(s_d.h, 1)
                            dve.wait_ge(s_q.h, s_q.at(i * 2))
                            for u in range(HALF):
                                dve.tensor_scalar(ohh[:, h, u, :], ioh[:, :], hi[:, bass.ds(c0 + u, 1)], None,
                                                  ALU.is_equal)
                                if weighted:
                                    ins = dve.tensor_scalar(ohl[:, h, u, :], ioh[:, 0:NB],
                                                            lo[:, bass.ds(c0 + u, 1)], wf[:, bass.ds(c0 + u, 1)],
                                                            ALU.is_equal, ALU.mult)
                                else:
                                    ins = dve.tensor_scalar(ohl[:, h, u, :], ioh[:, 0:NB],
                                                            lo[:, bass.ds(c0 + u, 1)], None, ALU.is_equal)
                            ins.then_inc(s_o.h, 1)
                        for h in range(2):
                            c0 = i * SLOTS + h * HALF
                            dve.wait_ge(s_b.h, s_b.at(i * 2 + h + 1))
                            dve.wait_ge(s_f.h, s_f.at(i * 2))
                            for u in range(HALF):
                                ins = dve.scalar_tensor_tensor(junk[:, h, u, :], pbc[:, h, u, :],
                                                               keyf[:, bass.ds(c0 + u, 1)], tri[:, :], ALU.is_equal,
                                                               ALU.mult, accum_out=before[:, bass.ds(c0 + u, 1)])
                            ins.then_inc(s_f.h, 1)
                    dve.wait_ge(s_f.h, s_f.at(2 * ITERS))
                    link(dve.tensor_scalar(before[:, :], before[:, :], 0.0, None, ALU.is_equal))
                    link(dve.tensor_scalar(tf[:, 0:T], keyf[:, 0:T], trash[:, 0:1], None, ALU.subtract))
                    link(dve.tensor_tensor(tf[:, 0:T], tf[:, 0:T], before[:, :], ALU.mult))
                    link(dve.tensor_scalar(tf[:, 0:T], tf[:, 0:T], trash[:, 0:1], None, ALU.add))
                    link(dve.memset(tf[:, T:TI], float(N)))
                    link(dve.tensor_copy(scat_i[:, :], tf[:, :]))
                    dve.wait_ge(s_t.h, s_t.at(1))
                    link(dve.tensor_copy(deg[:, :], pdeg[:, 0:NB]))

                @block.tensor
                def _(pe):
                    pe.wait_ge(s_x4.h, s_x4.at(2))
                    nc.tensor.matmul(pdeg[:, 0:NB], zero[:, :], zero[:, 0:NB], start=True, stop=False,
                                     skip_group_check=True)
                    with pe.Fori(0, ITERS) as i:
                        for h in range(2):
                            pe.wait_ge(s_f.h, s_f.at(i * 2))
                            pe.wait_ge(s_d.h, s_d.at(i * 2 + h + 1))
                            nc.tensor.matmul(pbc[:, h, :, :].rearrange("p u q -> p (u q)"), ones[:, :],
                                             diag[:, h, :, :].rearrange("p u q -> p (u q)"), start=True,
                                             stop=True).then_inc(s_b.h, 1)
                            pe.wait_ge(s_o.h, s_o.at(i * 2 + h + 1))
                            for u in range(HALF):
                                ins = nc.tensor.matmul(pdeg[:, 0:NB], ohh[:, h, u, :], ohl[:, h, u, :], start=False,
                                                       stop=False, skip_group_check=True)
                            ins.then_inc(s_q.h, 1)
                    nc.tensor.matmul(pdeg[:, 0:NB], zero[:, :], zero[:, 0:NB], start=False, stop=True,
                                     skip_group_check=True).then_inc(s_t.h, 1)

                for s in (s_d, s_b, s_f, s_o, s_q):
                    s.past(2 * ITERS)
                s_x4.past(2)
                s_t.past(1)

        s_diag = sem("diag_ready")
        s_bc = sem("keys_broadcast")
        index_stage(srcf, ssc_i, degs, True, s_diag, s_bc)
        index_stage(dstf, dsc_i, degd, False, s_diag, s_bc)

        with ExitStack() as c:
            block = c.enter_context(nc.Block())
            zn = [a for a in acc_n] + [a for l in acc for a in l]

            @block.vector
            def _(dve):
                link = linker(dve, s_v)
                dve.memset(Y[:, :, :], 0.0)
                dve.memset(Z[:, :, :], 0.0)
                dve.memset(V[:, :, :], -BIG).then_inc(s_x1.h, 1)

            @block.sync
            def _(sp):
                sp.wait_ge(s_x1.h, s_x1.at(1))
                zrow = Y[:, :, :].rearrange("p b d -> p (b d)")
                for a in zn:
                    w = a.shape[1]
                    if w == D:
                        sp.dma_start(a.rearrange("(p b) d -> p (b d)", b=NB), zrow).then_inc(s_st.h, 16)
                    else:
                        v = a.rearrange("(p b) d -> p (b d)", b=NB)
                        sp.dma_start(v[:, 0:NB * D], zrow).then_inc(s_st.h, 16)
                        sp.dma_start(v[:, NB * D:NB * w], zrow[:, 0:NB * (w - D)]).then_inc(s_st.h, 16)
                        s_st.past(16)
                for a in mx:
                    sp.dma_start(a.rearrange("(p b) d -> p (b d)", b=NB),
                                 V[:, :, :].rearrange("p b d -> p (b d)")[:, 0:NB * NH]).then_inc(s_st.h, 16)
                s_st.past(16 * (len(zn) + len(mx)))
                sp.wait_ge(s_st.h, s_st.base)

            s_x1.past(1)

        def ln_dve(dve, link, act_req, act_done, src, dst):
            link(dve.tensor_reduce(red[:, :], src[:, :, :], AX, ALU.add))
            link(dve.tensor_scalar(red[:, :], red[:, :], 1.0 / D, None, ALU.mult))
            link(dve.tensor_tensor(src[:, :, :], src[:, :, :], bc_last(red[:, :], D), ALU.subtract))
            link(dve.tensor_tensor(dst[:, :, :], src[:, :, :], src[:, :, :], ALU.mult))
            link(dve.tensor_reduce(red[:, :], dst[:, :, :], AX, ALU.add))
            dve.tensor_scalar(red[:, :], red[:, :], 1.0 / D, LN_EPS, ALU.mult, ALU.add).then_inc(act_req.h, 1)
            act_req.past(1)
            act_done.past(1)
            dve.wait_ge(act_done.h, act_done.base)
            link(dve.reciprocal(red[:, :], red2[:, :]))
            link(dve.tensor_tensor(dst[:, :, :], src[:, :, :], bc_last(red[:, :], D), ALU.mult))

        def sqrt_act(act, req, done, n):
            for k in range(1, n + 1):
                act.wait_ge(req.h, req.at(k))
                nc.scalar.activation(red2[:, :], red[:, :], ACT.Sqrt).then_inc(done.h, 1)

        s_rq = sem("variance_ready")
        s_sd = sem("root_ready")

        def dve_stage(body, rows=(), n_ln=0, act_extra=None):
            with ExitStack() as c:
                block = c.enter_context(nc.Block())
                nrow = len(rows)

                @block.sync
                def _(sp):
                    for k, r in enumerate(rows):
                        sp.dma_start(rowb[:, k, 0:r.shape[0]], r.unsqueeze(0).to_broadcast([P, r.shape[0]])).then_inc(s_ld.h, 16)

                @block.scalar
                def _(act):
                    sqrt_act(act, s_rq, s_sd, n_ln)

                @block.vector
                def _(dve):
                    link = linker(dve, s_v)
                    if nrow:
                        dve.wait_ge(s_ld.h, s_ld.at(16 * nrow))
                    body(dve, link)

                s_ld.past(16 * nrow)

        s_blk = sem("blocks_copied")
        s_tr = sem("blocks_transposed")
        s_trc = sem("transposes_copied")
        s_mm = sem("products_ready")
        s_ev = sem("products_copied")

        def node_mm(src, weights):
            steps = NB // GB
            with ExitStack() as c:
                xb = sb(c, "xb", [P, GB, D])
                xT = sb(c, "xT", [P, GB, P])
                width = max(w[0].shape[1] for w in weights)
                stage = sb(c, "stage", [P, GB, width])
                pT = ps(c, "pT", [P, 2, 4, P])
                pO = ps(c, "pO", [P, GB, 512])
                nw = len(weights)
                is_dram = [w[3] for w in weights]
                block = c.enter_context(nc.Block())

                @block.vector
                def _(dve):
                    with dve.Fori(0, steps) as i:
                        dve.wait_ge(s_tr.h, s_tr.at(i))
                        dve.tensor_copy(xb[:, :, :], src[:, bass.ds(i * GB, GB), :]).then_inc(s_blk.h, 1)

                @block.tensor
                def _(pe):
                    with pe.Fori(0, steps) as i:
                        pe.wait_ge(s_blk.h, s_blk.at(i + 1))
                        pe.wait_ge(s_trc.h, s_trc.at(i))
                        for g in range(GB):
                            ins = nc.tensor.transpose(pT[:, g // 4, g % 4, :], xb[:, g, :], ident[:, :])
                        ins.then_inc(s_tr.h, 1)
                        pe.wait_ge(s_trc.h, s_trc.at(i + 1))
                        for k, (rhs, dst, func, _d) in enumerate(weights):
                            pe.wait_ge(s_ev.h, s_ev.at(i * nw + k))
                            for g in range(GB):
                                ins = nc.tensor.matmul(pO[:, g, 0:rhs.shape[1]], xT[:, g, :], rhs, start=True,
                                                       stop=True)
                            ins.then_inc(s_mm.h, 1)

                @block.scalar
                def _(act):
                    with act.Fori(0, steps) as i:
                        act.wait_ge(s_tr.h, s_tr.at(i + 1))
                        act.wait_ge(s_mm.h, s_mm.at(i * nw))
                        nc.scalar.activation(xT[:, 0:4, :], pT[:, 0, :, :], ACT.Copy)
                        nc.scalar.activation(xT[:, 4:5, :], pT[:, 1, 0:1, :], ACT.Copy).then_inc(s_trc.h, 1)
                        for k, (rhs, dst, func, dr) in enumerate(weights):
                            w = rhs.shape[1]
                            act.wait_ge(s_mm.h, s_mm.at(i * nw + k + 1))
                            if dr:
                                nd = sum(is_dram)
                                done = sum(is_dram[0:k])
                                act.wait_ge(s_st.h, s_st.at(i * (16 * nd) + 16 * done))
                                nc.scalar.activation(stage[:, :, 0:w], pO[:, :, 0:w], func).then_inc(s_ev.h, 1)
                            else:
                                nc.scalar.activation(dst[:, bass.ds(i * GB, GB), :], pO[:, :, 0:w],
                                                     func).then_inc(s_ev.h, 1)

                @block.sync
                def _(sp):
                    if not any(is_dram):
                        return
                    with sp.Fori(0, steps) as i:
                        for k, (rhs, dst, func, dr) in enumerate(weights):
                            if dr:
                                w = rhs.shape[1]
                                sp.wait_ge(s_ev.h, s_ev.at(i * nw + k + 1))
                                sp.dma_start(dst[:, bass.ds(i * GB, GB), :], stage[:, :, 0:w]).then_inc(s_st.h, 16)
                    sp.wait_ge(s_st.h, s_st.at(16 * sum(is_dram) * steps))

                for s in (s_blk, s_tr, s_trc):
                    s.past(steps)
                for s in (s_mm, s_ev):
                    s.past(steps * nw)
                s_st.past(16 * sum(is_dram) * steps)

        def nodes(t):
            return t.rearrange("(p b) d -> p b d", b=NB)

        def load_store(pairs):
            with ExitStack() as c:
                block = c.enter_context(nc.Block())

                @block.sync
                def _(sp):
                    for a, b in pairs:
                        sp.dma_start(a, b).then_inc(s_st.h, 16)
                    sp.wait_ge(s_st.h, s_st.at(16 * len(pairs)))

                s_st.past(16 * len(pairs))

        def sum_tables(tabs, dst, tmp, lo=0, width=D):
            with ExitStack() as c:
                block = c.enter_context(nc.Block())
                n, nt = len(tabs), len(tmp)

                @block.sync
                def _(sp):
                    for k, t in enumerate(tabs):
                        if k > nt:
                            sp.wait_ge(s_x1.h, s_x1.at(k - nt))
                        to = dst if k == 0 else tmp[(k - 1) % nt]
                        sp.dma_start(to[:, :, 0:width], nodes(t)[:, :, lo:lo + width]).then_inc(tabsem[k].h, 16)

                @block.vector
                def _(dve):
                    for k in range(n):
                        dve.wait_ge(tabsem[k].h, tabsem[k].at(16))
                        if k:
                            dve.tensor_tensor(dst[:, :, 0:width], dst[:, :, 0:width], tmp[(k - 1) % nt][:, :, 0:width],
                                              ALU.add).then_inc(s_x1.h, 1)
                            dve.wait_ge(s_x1.h, s_x1.at(k))

                s_x1.past(n - 1)
                for k in range(n):
                    tabsem[k].past(16)

        tabsem = [sem(f"table{k}_landed") for k in range(TABLES)]
        g_landed = [sem(f"rows{s}_landed") for s in range(SLOTS)]
        g2_landed = [sem(f"rows_b{s}_landed") for s in range(SLOTS)]
        scattered = [sem(f"sums{s}_scattered") for s in range(SLOTS)]
        s_ix = [sem(f"indices{h}_ready") for h in range(2)]
        s_eq = sem("equality_ready")
        s_cmb = sem("combined")
        s_stg = sem("staged")
        s_sc2 = sem("scatter_indices_ready")

        bound = {}
        s_went = sem("pool_went_on")

        def carry():
            nc.gpsimd.sem_inc(s_went.h, 1)

        def set_bounds(pool, *tables):
            bound.clear()
            for t in tables:
                if t.shape[0] not in bound:
                    bound[t.shape[0]] = pool.to_reg(t.shape[0] - 1)

        def gather(dst, table, idx, s):
            nc.gpsimd.indirect_dma_start(dst, None, table, bass.IndirectOffsetOnAxis(ap=idx.bitcast(U32), axis=0),
                                         bounds_check=bound[table.shape[0]], oob_is_err=True).then_inc(s.h, 16)

        def scatter(table, idx, src, s, add=True):
            nc.gpsimd.indirect_dma_start(table, bass.IndirectOffsetOnAxis(ap=idx.bitcast(U32), axis=0), src, None,
                                         bounds_check=bound[table.shape[0]], oob_is_err=True,
                                         **({"compute_op": ALU.add} if add else {})).then_inc(s.h, 16)

        def spmm(table, gidx, keyf, scat_i, weighted, accs):
            with ExitStack() as c:
                gi = sb(c, "gi", [P, 2, HALF], I32)
                si = sb(c, "si", [P, 2, HALF], I32)
                G = sb(c, "G", [P, 2, HALF, D])
                diag = sb(c, "diag", [P, 2, HALF, P])
                eq = sb(c, "eq", [P, 2, HALF, P])
                stg = sb(c, "stg", [P, 2, HALF, D])
                pbc = ps(c, "pbc", [P, 2, HALF, P])
                pcm = ps(c, "pcm", [P, 2, HALF, D])
                block = c.enter_context(nc.Block())

                @block.scalar
                def _(act):
                    nc.scalar.activation(gi[:, 0, :], gidx[:, 0:HALF], ACT.Copy).then_inc(s_ix[0].h, 1)
                    with act.Fori(0, ITERS) as i:
                        for h in range(2):
                            g = 1 - h
                            for u in range(HALF):
                                k = i + 1 if g == 0 else i
                                act.wait_ge(g_landed[g * HALF + u].h, g_landed[g * HALF + u].at(k * 16))
                            nc.scalar.activation(gi[:, g, :], gidx[:, bass.ds(i * SLOTS + (h + 1) * HALF, HALF)],
                                                 ACT.Copy).then_inc(s_ix[g].h, 1)
                            for u in range(HALF):
                                act.wait_ge(scattered[h * HALF + u].h, scattered[h * HALF + u].at(i * 16))
                            nc.scalar.activation(si[:, h, :], scat_i[:, bass.ds(i * SLOTS + h * HALF, HALF)],
                                                 ACT.Copy)
                            act.wait_ge(s_cmb.h, s_cmb.at(i * 2 + h + 1))
                            nc.scalar.activation(stg[:, h, :, :], pcm[:, h, :, :], ACT.Copy).then_inc(s_stg.h, 1)

                @block.gpsimd
                def _(pool):
                    set_bounds(pool, table, accs[0])
                    pool.wait_ge(s_ix[0].h, s_ix[0].at(1))
                    for u in range(HALF):
                        gather(G[:, 0, u, :], table, gi[:, 0, u:u + 1], g_landed[u])
                    with pool.Fori(0, ITERS) as i:
                        for h in range(2):
                            g = 1 - h
                            k = i + 1 if g == 0 else i
                            pool.wait_ge(s_ix[g].h, s_ix[g].at(k + 1))
                            pool.wait_ge(s_cmb.h, s_cmb.at(i * 2 + h))
                            carry()
                            for u in range(HALF):
                                gather(G[:, g, u, :], table, gi[:, g, u:u + 1], g_landed[g * HALF + u])
                            pool.wait_ge(s_stg.h, s_stg.at(i * 2 + h + 1))
                            for u in range(HALF):
                                o = scattered[(1 - h) * HALF + u]
                                pool.wait_ge(o.h, o.at((i + h) * 16))
                            carry()
                            for u in range(HALF):
                                scatter(accs[u], si[:, h, u:u + 1], stg[:, h, u, :], scattered[h * HALF + u])
                    for s in range(SLOTS):
                        pool.wait_ge(scattered[s].h, scattered[s].at(16 * ITERS))
                    for u in range(HALF):
                        pool.wait_ge(g_landed[u].h, g_landed[u].at(16 * (ITERS + 1)))

                @block.vector
                def _(dve):
                    with dve.Fori(0, ITERS) as i:
                        for h in range(2):
                            c0 = i * SLOTS + h * HALF
                            dve.wait_ge(s_bc.h, s_bc.at(i * 2))
                            dve.tensor_tensor(diag[:, h, :, :], bc_mid(ident[:, :], HALF),
                                              bc_last(keyf[:, bass.ds(c0, HALF)], P), ALU.mult).then_inc(s_diag.h, 1)
                            dve.wait_ge(s_bc.h, s_bc.at(i * 2 + h + 1))
                            dve.wait_ge(s_cmb.h, s_cmb.at(i * 2))
                            for u in range(HALF):
                                key = keyf[:, bass.ds(c0 + u, 1)]
                                if weighted:
                                    ins = dve.tensor_scalar(eq[:, h, u, :], pbc[:, h, u, :], key,
                                                            wf[:, bass.ds(c0 + u, 1)], ALU.is_equal, ALU.mult)
                                else:
                                    ins = dve.tensor_scalar(eq[:, h, u, :], pbc[:, h, u, :], key, None, ALU.is_equal)
                            ins.then_inc(s_eq.h, 1)

                @block.tensor
                def _(pe):
                    with pe.Fori(0, ITERS) as i:
                        for h in range(2):
                            pe.wait_ge(s_diag.h, s_diag.at(i * 2 + h + 1))
                            pe.wait_ge(s_eq.h, s_eq.at(i * 2))
                            nc.tensor.matmul(pbc[:, h, :, :].rearrange("p u q -> p (u q)"), ones[:, :],
                                             diag[:, h, :, :].rearrange("p u q -> p (u q)"), start=True,
                                             stop=True).then_inc(s_bc.h, 1)
                            pe.wait_ge(s_eq.h, s_eq.at(i * 2 + h + 1))
                            pe.wait_ge(s_stg.h, s_stg.at(i * 2))
                            for u in range(HALF):
                                pe.wait_ge(g_landed[h * HALF + u].h, g_landed[h * HALF + u].at(i * 16 + 16))
                                ins = nc.tensor.matmul(pcm[:, h, u, :], eq[:, h, u, :], G[:, h, u, :], start=True,
                                                       stop=True)
                            ins.then_inc(s_cmb.h, 1)

                for s in (s_diag, s_bc, s_eq, s_cmb, s_stg):
                    s.past(2 * ITERS)
                s_ix[0].past(ITERS + 1)
                s_ix[1].past(ITERS)
                for s in range(SLOTS):
                    g_landed[s].past(16 * (ITERS + (s < HALF)))
                    scattered[s].past(16 * ITERS)

        def wt(name, w, dt=F32):
            return sb(top, name, [P, w], dt)

        w_kv, w_q, w_vl, w_out = wt("w_kv", 2 * D), wt("w_q", QW), wt("w_vl", D), wt("w_out", D)
        w_p, w_self = wt("w_p", D), wt("w_self", D)
        w_g = [wt(f"w_g{k}", D) for k in range(3)]
        w_n1, w_n2 = wt("w_n1", D), wt("w_n2", D)
        w_rel = wt("w_rel", NT * D)
        w1 = sb(top, "w1", [2 * EC, 4 * KH])
        b1 = sb(top, "b1", [4 * KH, 1])
        w2 = sb(top, "w2", [4 * KH, 4 * KH])
        b2 = sb(top, "b2", [1, 4 * KH])
        with ExitStack() as c:
            qn, ql = sb(c, "qn", [P, D]), sb(c, "ql", [P, QW])
            nat = [sb(c, f"nat{k}", [P, D]) for k in range(3)]
            wbas = sb(c, "wbas", [P, NBAS, D])
            alf = sb(c, "alf", [P, NT, NBAS])
            wtmp = sb(c, "wtmp", [P, NT, D])
            pw = ps(c, "pw", [P, 4, 512])
            block = c.enter_context(nc.Block())
            n_w = 6 * NH + 26

            @block.vector
            def _(dve):
                link = linker(dve, s_v)
                for t in (w_kv, qn, ql, w_vl):
                    dve.memset(t[:, :], 0.0)
                dve.memset(w1[:, :], 0.0)
                dve.memset(w2[:, :], 0.0).then_inc(s_x1.h, 1)
                dve.wait_ge(s_ld.h, s_ld.at(16 * n_w))
                rel = w_rel[:, :].rearrange("p (t d) -> p t d", t=NT)
                for b in range(NBAS):
                    dst = rel if b == 0 else wtmp[:, :, :]
                    link(dve.tensor_tensor(dst, bc_mid(wbas[:, b, :], NT), bc_last(alf[:, :, b], D), ALU.mult))
                    if b:
                        link(dve.tensor_tensor(rel, rel, wtmp[:, :, :], ALU.add))
                dve.wait_ge(s_t.h, s_t.at(4))
                link(dve.tensor_copy(w_q[:, :], pw[:, 0, 0:QW]))
                for k, t in enumerate((w_out, w_n1, w_n2)):
                    link(dve.tensor_copy(t[:, :], pw[:, 1 + k, 0:D]))

            @block.sync
            def _(sp):
                n = [0]

                def ld(dst, src):
                    n[0] += 1
                    sp.dma_start(dst, src).then_inc(s_ld.h, 16)

                sp.wait_ge(s_x1.h, s_x1.at(1))
                with nc.allow_non_contiguous_dma(reason="small transposed weights"):
                    for h in range(NH):
                        r = slice(h * KH, (h + 1) * KH)
                        ld(w_kv[r, r], I["L0_gnn_k_w"][h].rearrange("k d -> d k"))
                        ld(w_kv[r, D + h * KH:D + (h + 1) * KH], I["L0_gnn_v_w"][h].rearrange("k d -> d k"))
                        ld(qn[r, r], I["L0_gnn_q_w"][h])
                        ld(ql[r, r], I["L0_gnn_wkl_w"])
                        ld(ql[r, D + h:D + h + 1], I["L0_gnn_wkl_b"].unsqueeze(1))
                        ld(w_vl[r, r], I["L0_gnn_wvl_w"].rearrange("k d -> d k"))
                    for j in range(2):
                        e0, k0 = j * EC, j * 2 * KH
                        k1, k2 = k0 + KH, k0 + 2 * KH
                        ld(w1[e0:e0 + EC, k0:k1], I["L0_gnn_wk1_w"].rearrange("k d -> d k"))
                        ld(w1[e0:e0 + EC, k1:k2], I["L0_gnn_wv1_w"].rearrange("k d -> d k"))
                        ld(b1[k0:k1, :], I["L0_gnn_wk1_b"].unsqueeze(1))
                        ld(b1[k1:k2, :], I["L0_gnn_wv1_b"].unsqueeze(1))
                        ld(w2[k0:k1, k0:k1], I["L0_gnn_wk2_w"].rearrange("k d -> d k"))
                        ld(w2[k1:k2, k1:k2], I["L0_gnn_wv2_w"].rearrange("k d -> d k"))
                        ld(b2[:, k0:k1], I["L0_gnn_wk2_b"].unsqueeze(0))
                        ld(b2[:, k1:k2], I["L0_gnn_wv2_b"].unsqueeze(0))
                    for t, src in ((nat[0], "L0_gnn_out_w"), (nat[1], "L2_gnn_W1"), (nat[2], "L2_gnn_W2"),
                                   (w_p, "L1_gnn_Wp"), (w_g[0], "L1_gnn_W0"), (w_g[1], "L1_gnn_W1"),
                                   (w_g[2], "L1_gnn_W2"), (w_self, "L3_gnn_w_self")):
                        ld(t[:, :], I[src])
                    ld(wbas[:, :, :], I["L3_gnn_weight"].rearrange("b i o -> i b o"))
                    ld(alf[:, :, :].rearrange("p t b -> p (t b)"),
                       I["L3_gnn_alpha"].rearrange("t b -> (t b)").unsqueeze(0).to_broadcast([P, NT * NBAS]))
                n_loads.append(n[0])

            @block.tensor
            def _(pe):
                pe.wait_ge(s_ld.h, s_ld.at(16 * n_w))
                nc.tensor.matmul(pw[:, 0, 0:QW], qn[:, :], ql[:, :], start=True, stop=True).then_inc(s_t.h, 1)
                for k in range(3):
                    nc.tensor.transpose(pw[:, 1 + k, 0:D], nat[k][:, :], ident[:, :]).then_inc(s_t.h, 1)

            assert n_loads[-1] == n_w, n_loads
            s_x1.past(1)
            s_t.past(4)
            s_ld.past(16 * n_w)

        def affine(dve, link, t, k_mul, k_add):
            if k_mul is not None:
                link(dve.tensor_tensor(t[:, :, :], t[:, :, :], bc_mid(rowb[:, k_mul, :], NB), ALU.mult))
            link(dve.tensor_tensor(t[:, :, :], t[:, :, :], bc_mid(rowb[:, k_add, :], NB), ALU.add))

        def pre0(dve, link):
            link(dve.tensor_copy(V[:, :, :], X[:, :, :]))
            ln_dve(dve, link, s_rq, s_sd, V, Y)
            affine(dve, link, Y, 0, 1)

        dve_stage(pre0, rows=(I["L0_gnn_ln1_g"], I["L0_gnn_ln1_b"]), n_ln=1)
        node_mm(Y, [(w_kv[:, :], nodes(kv_t), ACT.Copy, True), (w_q[:, :], nodes(q_t), ACT.Copy, True)])

        qkA = sb(top, "qkA", [P, T, NH])
        attr_landed = [sem(f"attr{h}_landed") for h in range(2)]
        u_moved = [sem(f"products{h}_moved") for h in range(2)]
        s_aT = sem("attr_transposed")
        s_aTc = sem("attr_copied")
        s_hid = sem("hidden_sums")
        s_rel = sem("relu_ready")
        s_lg = sem("log_ready")
        s_hr = sem("hidden_ready")
        s_W = sem("edge_weights_ready")
        s_u = sem("products_made")

        with ExitStack() as c:
            gk, gq = sb(c, "gk", [P, 2, HALF], I32), sb(c, "gq", [P, 2, HALF], I32)
            KV, Q = sb(c, "KV", [P, 2, HALF, 2 * D]), sb(c, "Q", [P, 2, HALF, QW])
            at = sb(c, "at", [P, 2, HALF, EC])
            aT = sb(c, "aT", [2 * EC, 2, HALF // 2 * P])
            sa, se, sl, sr, hid = [sb(c, n, [4 * KH, HALF // 2 * P]) for n in ("sa", "se", "sl", "sr", "hid")]
            t1, t2 = sb(c, "t1", [P, HALF, D]), sb(c, "t2", [P, HALF, D])
            U = sb(c, "U", [P, 2, HALF, D])
            pA, pH = ps(c, "pA", [2 * EC, HALF // 2, P]), ps(c, "pH", [4 * KH, HALF // 2 * P])
            pW = ps(c, "pW", [P, HALF, 2 * KH])
            attr = over(I["edge_attr_64"], EC)
            block = c.enter_context(nc.Block())

            @block.sync
            def _(sp):
                with sp.Fori(0, ITERS) as i:
                    for h in range(2):
                        sp.wait_ge(s_aT.h, s_aT.at(i * 2))
                        sp.dma_start(at[:, h, :, :].rearrange("p u d -> p (u d)"),
                                     attr[:, bass.ds((i * SLOTS + h * HALF) * EC, HALF * EC)])\
                            .then_inc(attr_landed[h].h, 16)
                    for h in range(2):
                        sp.wait_ge(s_u.h, s_u.at(i * 2 + h + 1))
                        sp.dma_start(u_d[:, bass.ds((i * SLOTS + h * HALF) * D, HALF * D)],
                                     U[:, h, :, :].rearrange("p u d -> p (u d)")).then_inc(u_moved[h].h, 16)
                for h in range(2):
                    sp.wait_ge(u_moved[h].h, u_moved[h].at(16 * ITERS))

            @block.gpsimd
            def _(pool):
                set_bounds(pool, kv_t)
                with pool.Fori(0, ITERS) as i:
                    for h in range(2):
                        pool.wait_ge(s_ix[h].h, s_ix[h].at(i + 1))
                        pool.wait_ge(s_u.h, s_u.at(i * 2))
                        carry()
                        for u in range(HALF):
                            gather(KV[:, h, u, :], kv_t, gk[:, h, u:u + 1], g_landed[h * HALF + u])
                            gather(Q[:, h, u, :], q_t, gq[:, h, u:u + 1], g2_landed[h * HALF + u])

            @block.scalar
            def _(act):
                with act.Fori(0, ITERS) as i:
                    for h in range(2):
                        for u in range(HALF):
                            act.wait_ge(g_landed[h * HALF + u].h, g_landed[h * HALF + u].at(16 * i))
                            act.wait_ge(g2_landed[h * HALF + u].h, g2_landed[h * HALF + u].at(16 * i))
                        cols = bass.ds(i * SLOTS + h * HALF, HALF)
                        nc.scalar.activation(gk[:, h, :], dst_i[:, cols], ACT.Copy)
                        nc.scalar.activation(gq[:, h, :], src_i[:, cols], ACT.Copy).then_inc(s_ix[h].h, 1)
                    for h in range(2):
                        n = i * 2 + h
                        act.wait_ge(s_aT.h, s_aT.at(n + 1))
                        act.wait_ge(s_hid.h, s_hid.at(i * 2))
                        nc.scalar.activation(aT[:, h, :], pA[:, :, :].rearrange("p u q -> p (u q)"),
                                             ACT.Copy).then_inc(s_aTc.h, 1)
                        act.wait_ge(s_hid.h, s_hid.at(n + 1))
                        act.wait_ge(s_rel.h, s_rel.at(n + 1))
                        nc.scalar.activation(sa[:, :], pH[:, :], ACT.Abs, bias=b1[:, 0:1]).then_inc(s_a.h, 1)
                        act.wait_ge(s_a.h, s_a.at(n * 2 + 1))
                        nc.scalar.activation(se[:, :], sa[:, :], ACT.Exp, scale=-1.0).then_inc(s_a.h, 1)
                        act.wait_ge(s_a.h, s_a.at(n * 2 + 2))
                        act.wait_ge(s_hr.h, s_hr.at(n))
                        nc.scalar.activation(sl[:, :], se[:, :], ACT.Ln, scale=0.5,
                                             bias=halfc[:, 0:1]).then_inc(s_lg.h, 1)

            @block.tensor
            def _(pe):
                with pe.Fori(0, ITERS) as i:
                    for h in range(2):
                        n = i * 2 + h
                        pe.wait_ge(attr_landed[h].h, attr_landed[h].at(i * 16 + 16))
                        pe.wait_ge(s_aTc.h, s_aTc.at(n))
                        for g in range(HALF // 2):
                            ins = nc.tensor.transpose(pA[:, g, :],
                                                      at[:, h, 2 * g:2 * g + 2, :].rearrange("p u d -> p (u d)"),
                                                      ident[:, :])
                        ins.then_inc(s_aT.h, 1)
                        pe.wait_ge(s_aTc.h, s_aTc.at(n + 1))
                        pe.wait_ge(s_rel.h, s_rel.at(n))
                        pe.wait_ge(s_lg.h, s_lg.at(n))
                        nc.tensor.matmul(pH[:, :], w1[:, :], aT[:, h, :], start=True, stop=True).then_inc(s_hid.h, 1)
                        pe.wait_ge(s_hr.h, s_hr.at(n + 1))
                        pe.wait_ge(s_u.h, s_u.at(n))
                        for g in range(HALF // 2):
                            o = pW[:, 2 * g:2 * g + 2, :].rearrange("p u k -> p (u k)")
                            nc.tensor.matmul(o, hid[:, g * P:(g + 1) * P], w2[:, :], start=True, stop=False)
                            ins = nc.tensor.matmul(o, ones[0:1, :], b2[:, :], start=False, stop=True)
                        ins.then_inc(s_W.h, 1)

            @block.vector
            def _(dve):
                with dve.Fori(0, ITERS) as i:
                    for h in range(2):
                        n = i * 2 + h

                        def link(ins, j):
                            ins.then_inc(s_v.h, 1)
                            dve.wait_ge(s_v.h, s_v.at(n * 4 + j))

                        dve.wait_ge(s_hid.h, s_hid.at(n + 1))
                        dve.tensor_scalar(sr[:, :], pH[:, :], b1[:, 0:1], 0.0, ALU.add, ALU.max).then_inc(s_rel.h, 1)
                        dve.wait_ge(s_lg.h, s_lg.at(n + 1))
                        dve.wait_ge(s_rel.h, s_rel.at(n + 1))
                        dve.wait_ge(s_W.h, s_W.at(n))
                        dve.tensor_tensor(hid[:, :], sr[:, :], sl[:, :], ALU.add).then_inc(s_hr.h, 1)
                        for u in range(HALF):
                            dve.wait_ge(g_landed[h * HALF + u].h, g_landed[h * HALF + u].at(16 * i + 16))
                            dve.wait_ge(g2_landed[h * HALF + u].h, g2_landed[h * HALF + u].at(16 * i + 16))
                        link(dve.tensor_tensor(t1[:, :, :], KV[:, h, :, 0:D], Q[:, h, :, 0:D], ALU.mult), 1)
                        dve.wait_ge(s_W.h, s_W.at(n + 1))
                        for u in range(HALF):
                            ins = dve.tensor_tensor(t2[:, u, :].rearrange("p (h k) -> p h k", h=NH),
                                                    t1[:, u, :].rearrange("p (h k) -> p h k", h=NH),
                                                    bc_mid(pW[:, u, 0:KH], NH), ALU.mult)
                        link(ins, 2)
                        scores = qkA[:, bass.ds(i * SLOTS + h * HALF, HALF), :]
                        link(dve.tensor_reduce(scores, t2[:, :, :].rearrange("p u (h k) -> p u h k", h=NH), AX,
                                               ALU.add), 3)
                        link(dve.tensor_tensor(scores, scores, Q[:, h, :, D:QW], ALU.add), 4)
                        dve.wait_ge(u_moved[h].h, u_moved[h].at(16 * i))
                        for u in range(HALF):
                            ins = dve.tensor_tensor(U[:, h, u, :].rearrange("p (h k) -> p h k", h=NH),
                                                    KV[:, h, u, D:2 * D].rearrange("p (h k) -> p h k", h=NH),
                                                    bc_mid(pW[:, u, KH:2 * KH], NH), ALU.mult)
                        ins.then_inc(s_u.h, 1)

            for s in (s_aT, s_aTc, s_hid, s_lg, s_rel, s_hr, s_W, s_u):
                s.past(2 * ITERS)
            s_a.past(4 * ITERS)
            s_v.past(8 * ITERS)
            for h in range(2):
                s_ix[h].past(ITERS)
                attr_landed[h].past(16 * ITERS)
                u_moved[h].past(16 * ITERS)
            for s in range(SLOTS):
                g_landed[s].past(16 * ITERS)
                g2_landed[s].past(16 * ITERS)

        s_dq = sem("score_diagonals_ready")
        s_bq = sem("scores_broadcast")
        s_val = sem("scores_masked")
        s_new = sem("maxima_ready")
        with ExitStack() as c:
            gi, si = sb(c, "gi", [P, 2, HALF], I32), sb(c, "si", [P, 2, HALF], I32)
            cur, new = sb(c, "cur", [P, 2, HALF, NH]), sb(c, "new", [P, 2, HALF, NH])
            seg = sb(c, "seg", [P, HALF, NH])
            diag = sb(c, "diag", [P, HALF, P])
            dq = sb(c, "dq", [P, HALF * NH, P])
            mask = sb(c, "mask", [P, HALF, P])
            val = sb(c, "val", [P, HALF, NH, P])
            pbc, pbq = ps(c, "pbc", [P, HALF, P]), ps(c, "pbq", [P, HALF, NH, P])
            block = c.enter_context(nc.Block())

            @block.scalar
            def _(act):
                with act.Fori(0, ITERS) as i:
                    for h in range(2):
                        for u in range(HALF):
                            act.wait_ge(scattered[h * HALF + u].h, scattered[h * HALF + u].at(16 * i))
                        cols = bass.ds(i * SLOTS + h * HALF, HALF)
                        nc.scalar.activation(gi[:, h, :], src_i[:, cols], ACT.Copy)
                        nc.scalar.activation(si[:, h, :], ssc_i[:, cols], ACT.Copy).then_inc(s_ix[h].h, 1)

            @block.gpsimd
            def _(pool):
                set_bounds(pool, kv_t)
                with pool.Fori(0, ITERS) as i:
                    for h in range(2):
                        pool.wait_ge(s_ix[h].h, s_ix[h].at(i + 1))
                        carry()
                        for u in range(HALF):
                            s = h * HALF + u
                            gather(cur[:, h, u, :], mx[s], gi[:, h, u:u + 1], g_landed[s])
                    for h in range(2):
                        pool.wait_ge(s_new.h, s_new.at(i * 2 + h + 1))
                        carry()
                        for u in range(HALF):
                            s = h * HALF + u
                            scatter(mx[s], si[:, h, u:u + 1], new[:, h, u, :], scattered[s], add=False)
                for s in range(SLOTS):
                    pool.wait_ge(scattered[s].h, scattered[s].at(16 * ITERS))

            @block.tensor
            def _(pe):
                with pe.Fori(0, ITERS) as i:
                    for h in range(2):
                        n = i * 2 + h
                        pe.wait_ge(s_dq.h, s_dq.at(n + 1))
                        pe.wait_ge(s_val.h, s_val.at(n))
                        nc.tensor.matmul(pbc[:, :, :].rearrange("p u q -> p (u q)"), ones[:, :],
                                         diag[:, :, :].rearrange("p u q -> p (u q)"), start=True, stop=True)
                        for u in range(HALF):
                            ins = nc.tensor.matmul(pbq[:, u, :, :].rearrange("p h q -> p (h q)"), ones[:, :],
                                                   dq[:, u * NH:(u + 1) * NH, :].rearrange("p h q -> p (h q)"),
                                                   start=True, stop=True)
                        ins.then_inc(s_bq.h, 1)

            @block.vector
            def _(dve):
                with dve.Fori(0, ITERS) as i:
                    for h in range(2):
                        n = i * 2 + h

                        def link(ins, j):
                            ins.then_inc(s_v.h, 1)
                            dve.wait_ge(s_v.h, s_v.at(n * 2 + j))

                        c0 = i * SLOTS + h * HALF
                        dve.tensor_tensor(diag[:, :, :], bc_mid(ident[:, :], HALF),
                                          bc_last(srcf[:, bass.ds(c0, HALF)], P), ALU.mult)
                        dve.tensor_tensor(dq[:, :, :], bc_mid(ident[:, :], HALF * NH),
                                          bc_last(qkA[:, bass.ds(c0, HALF), :].rearrange("p u h -> p (u h)"), P),
                                          ALU.mult).then_inc(s_dq.h, 1)
                        dve.wait_ge(s_bq.h, s_bq.at(n + 1))
                        for u in range(HALF):
                            ins = dve.tensor_scalar(mask[:, u, :], pbc[:, u, :], srcf[:, bass.ds(c0 + u, 1)], -BIG,
                                                    ALU.not_equal, ALU.mult)
                        link(ins, 1)
                        for u in range(HALF):
                            ins = dve.tensor_tensor(val[:, u, :, :], pbq[:, u, :, :], bc_mid(mask[:, u, :], NH),
                                                    ALU.add)
                        ins.then_inc(s_val.h, 1)
                        dve.wait_ge(s_val.h, s_val.at(n + 1))
                        link(dve.tensor_reduce(seg[:, :, :], val[:, :, :, :], AX, ALU.max), 2)
                        for u in range(HALF):
                            dve.wait_ge(g_landed[h * HALF + u].h, g_landed[h * HALF + u].at(16 * i + 16))
                            dve.wait_ge(scattered[h * HALF + u].h, scattered[h * HALF + u].at(16 * i))
                        dve.tensor_tensor(new[:, h, :, :], seg[:, :, :], cur[:, h, :, :], ALU.max)\
                            .then_inc(s_new.h, 1)

            for s in (s_dq, s_bq, s_val, s_new):
                s.past(2 * ITERS)
            s_v.past(4 * ITERS)
            for h in range(2):
                s_ix[h].past(ITERS)
            for s in range(SLOTS):
                g_landed[s].past(16 * ITERS)
                scattered[s].past(16 * ITERS)

        with ExitStack() as c:
            mt = sb(c, "mt", [P, MTABLES, NB * NH])
            block = c.enter_context(nc.Block())

            @block.sync
            def _(sp):
                for k in range(MTABLES):
                    sp.dma_start(mt[:, k, :], mx[k].rearrange("(p b) d -> p (b d)", b=NB)).then_inc(s_ld.h, 16)
                sp.wait_ge(s_x1.h, s_x1.at(MTABLES - 1))
                sp.dma_start(m_t.rearrange("(p b) d -> p (b d)", b=NB), mt[:, 0, :]).then_inc(s_st.h, 16)
                sp.wait_ge(s_st.h, s_st.at(16))

            @block.vector
            def _(dve):
                dve.wait_ge(s_ld.h, s_ld.at(16 * MTABLES))
                for k in range(1, MTABLES):
                    dve.tensor_tensor(mt[:, 0, :], mt[:, 0, :], mt[:, k, :], ALU.max).then_inc(s_x1.h, 1)
                    dve.wait_ge(s_x1.h, s_x1.at(k))

            s_ld.past(16 * MTABLES)
            s_x1.past(MTABLES - 1)
            s_st.past(16)

        s_df = sem("differences_ready")
        s_ex = sem("exponentials_ready")
        s_row = sem("message_rows_ready")
        with ExitStack() as c:
            gi, si = sb(c, "gi", [P, 2, HALF], I32), sb(c, "si", [P, 2, HALF], I32)
            mg = sb(c, "mg", [P, 2, HALF, NH])
            df, ex = sb(c, "df", [P, 2, HALF, NH]), sb(c, "ex", [P, 2, HALF, NH])
            U, R = sb(c, "U", [P, 2, HALF, D]), sb(c, "R", [P, 2, HALF, QW])
            diag, eq = sb(c, "diag", [P, 2, HALF, P]), sb(c, "eq", [P, 2, HALF, P])
            stg = sb(c, "stg", [P, 2, HALF, QW])
            pbc, pcm = ps(c, "pbc", [P, 2, HALF, P]), ps(c, "pcm", [P, 2, HALF, 256])
            block = c.enter_context(nc.Block())

            @block.sync
            def _(sp):
                with sp.Fori(0, ITERS) as i:
                    for h in range(2):
                        sp.wait_ge(s_row.h, s_row.at(i * 2))
                        sp.dma_start(U[:, h, :, :].rearrange("p u d -> p (u d)"),
                                     u_d[:, bass.ds((i * SLOTS + h * HALF) * D, HALF * D)])\
                            .then_inc(u_moved[h].h, 16)

            @block.gpsimd
            def _(pool):
                set_bounds(pool, kv_t)
                with pool.Fori(0, ITERS) as i:
                    for h in range(2):
                        pool.wait_ge(s_ix[h].h, s_ix[h].at(i + 1))
                        pool.wait_ge(s_df.h, s_df.at(i * 2))
                        carry()
                        for u in range(HALF):
                            gather(mg[:, h, u, :], m_t, gi[:, h, u:u + 1], g_landed[h * HALF + u])
                    for h in range(2):
                        pool.wait_ge(s_stg.h, s_stg.at(i * 2 + h + 1))
                        for u in range(HALF):
                            o = scattered[(1 - h) * HALF + u]
                            pool.wait_ge(o.h, o.at((i + h) * 16))
                        carry()
                        for u in range(HALF):
                            scatter(acc_n[u], si[:, h, u:u + 1], stg[:, h, u, :], scattered[h * HALF + u])
                for s in range(SLOTS):
                    pool.wait_ge(scattered[s].h, scattered[s].at(16 * ITERS))

            @block.scalar
            def _(act):
                with act.Fori(0, ITERS) as i:
                    for h in range(2):
                        for u in range(HALF):
                            act.wait_ge(scattered[h * HALF + u].h, scattered[h * HALF + u].at(16 * i))
                        cols = bass.ds(i * SLOTS + h * HALF, HALF)
                        nc.scalar.activation(si[:, h, :], ssc_i[:, cols], ACT.Copy)
                        nc.scalar.activation(gi[:, h, :], src_i[:, cols], ACT.Copy).then_inc(s_ix[h].h, 1)
                    for h in range(2):
                        act.wait_ge(s_df.h, s_df.at(i * 2 + h + 1))
                        act.wait_ge(s_row.h, s_row.at(i * 2))
                        nc.scalar.activation(ex[:, h, :, :], df[:, h, :, :], ACT.Exp).then_inc(s_ex.h, 1)
                    for h in range(2):
                        act.wait_ge(s_cmb.h, s_cmb.at(i * 2 + h + 1))
                        nc.scalar.activation(stg[:, h, :, :], pcm[:, h, :, 0:QW], ACT.Copy).then_inc(s_stg.h, 1)

            @block.vector
            def _(dve):
                with dve.Fori(0, ITERS) as i:
                    for h in range(2):
                        c0 = i * SLOTS + h * HALF
                        dve.wait_ge(s_bc.h, s_bc.at(i * 2))
                        dve.tensor_tensor(diag[:, h, :, :], bc_mid(ident[:, :], HALF),
                                          bc_last(srcf[:, bass.ds(c0, HALF)], P), ALU.mult).then_inc(s_diag.h, 1)
                        for u in range(HALF):
                            dve.wait_ge(g_landed[h * HALF + u].h, g_landed[h * HALF + u].at(16 * i + 16))
                        dve.wait_ge(s_ex.h, s_ex.at(i * 2))
                        dve.tensor_tensor(df[:, h, :, :], qkA[:, bass.ds(c0, HALF), :], mg[:, h, :, :],
                                          ALU.subtract).then_inc(s_df.h, 1)
                        dve.wait_ge(s_bc.h, s_bc.at(i * 2 + h + 1))
                        dve.wait_ge(s_cmb.h, s_cmb.at(i * 2))
                        for u in range(HALF):
                            ins = dve.tensor_scalar(eq[:, h, u, :], pbc[:, h, u, :],
                                                    srcf[:, bass.ds(c0 + u, 1)], None, ALU.is_equal)
                        ins.then_inc(s_eq.h, 1)
                        dve.wait_ge(s_ex.h, s_ex.at(i * 2 + h + 1))
                        dve.wait_ge(u_moved[h].h, u_moved[h].at(16 * i + 16))
                        dve.tensor_copy(R[:, h, :, D:QW], ex[:, h, :, :])
                        for u in range(HALF):
                            ins = dve.tensor_tensor(R[:, h, u, 0:D].rearrange("p (h k) -> p h k", h=NH),
                                                    U[:, h, u, :].rearrange("p (h k) -> p h k", h=NH),
                                                    bc_last(ex[:, h, u, :], KH), ALU.mult)
                        ins.then_inc(s_row.h, 1)

            @block.tensor
            def _(pe):
                with pe.Fori(0, ITERS) as i:
                    for h in range(2):
                        pe.wait_ge(s_diag.h, s_diag.at(i * 2 + h + 1))
                        pe.wait_ge(s_eq.h, s_eq.at(i * 2))
                        nc.tensor.matmul(pbc[:, h, :, :].rearrange("p u q -> p (u q)"), ones[:, :],
                                         diag[:, h, :, :].rearrange("p u q -> p (u q)"), start=True,
                                         stop=True).then_inc(s_bc.h, 1)
                        pe.wait_ge(s_eq.h, s_eq.at(i * 2 + h + 1))
                        pe.wait_ge(s_row.h, s_row.at(i * 2 + h + 1))
                        pe.wait_ge(s_stg.h, s_stg.at(i * 2))
                        for u in range(HALF):
                            ins = nc.tensor.matmul(pcm[:, h, u, 0:QW], eq[:, h, u, :], R[:, h, u, :], start=True,
                                                   stop=True)
                        ins.then_inc(s_cmb.h, 1)

            for s in (s_diag, s_bc, s_eq, s_cmb, s_stg, s_df, s_ex, s_row):
                s.past(2 * ITERS)
            for h in range(2):
                s_ix[h].past(ITERS)
                u_moved[h].past(16 * ITERS)
            for s in range(SLOTS):
                g_landed[s].past(16 * ITERS)
                scattered[s].past(16 * ITERS)

        den = sb(top, "den", [P, NB, NH])
        dt0, dt1 = sb(top, "dt0", [P, NB, NH]), sb(top, "dt1", [P, NB, NH])
        sum_tables(acc_n, Y, (Z, V))
        sum_tables(acc_n, den, (dt0, dt1), D, NH)

        def heads(t):
            return t[:, :, :].rearrange("p b (h k) -> p (b h) k", h=NH)

        def flat(t):
            return t[:, :, :].rearrange("p b h -> p (b h)")

        def norm0(dve, link):
            link(dve.tensor_scalar(flat(dt0), flat(den), 1e-30, None, ALU.max))
            link(dve.reciprocal(flat(dt0), flat(dt0)))
            link(dve.tensor_tensor(flat(dt1), flat(den), flat(dt0), ALU.mult))
            link(dve.tensor_tensor(heads(Y), heads(Y), bc_last(flat(dt0), KH), ALU.mult))

        dve_stage(norm0)
        node_mm(Y, [(w_vl[:, :], Z, ACT.Copy, False)])

        def mid0(dve, link):
            for h in range(NH):
                link(dve.tensor_tensor(V[:, :, h * KH:(h + 1) * KH], bc_mid(rowb[:, 2, 0:KH], NB),
                                       bc_last(dt1[:, :, h], KH), ALU.mult))
            link(dve.tensor_tensor(Z[:, :, :], Z[:, :, :], V[:, :, :], ALU.add))
            link(dve.tensor_tensor(Z[:, :, :], Z[:, :, :], X[:, :, :], ALU.add))
            link(dve.tensor_copy(V[:, :, :], Z[:, :, :]))
            ln_dve(dve, link, s_rq, s_sd, V, Y)
            affine(dve, link, Y, 0, 1)

        dve_stage(mid0, rows=(I["L0_gnn_ln2_g"], I["L0_gnn_ln2_b"], I["L0_gnn_wvl_b"]), n_ln=1)

        def act_stage(body):
            with ExitStack() as c:
                block = c.enter_context(nc.Block())

                @block.scalar
                def _(act):
                    body(act, linker(act, s_a))

        def ssp0(act, link):
            link(nc.scalar.activation(V[:, :, :], Y[:, :, :], ACT.Abs))
            link(nc.scalar.activation(V[:, :, :], V[:, :, :], ACT.Exp, scale=-1.0))
            link(nc.scalar.activation(V[:, :, :], V[:, :, :], ACT.Ln, scale=0.5, bias=halfc[:, 0:1]))

        act_stage(ssp0)

        def hid0(dve, link):
            link(dve.scalar_tensor_tensor(Y[:, :, :], Y[:, :, :], 0.0, V[:, :, :], ALU.max, ALU.add))

        dve_stage(hid0)
        node_mm(Y, [(w_out[:, :], V, ACT.Copy, False)])

        def post0(dve, link):
            affine(dve, link, V, None, 0)
            link(dve.tensor_tensor(V[:, :, :], V[:, :, :], Z[:, :, :], ALU.add))
            link(dve.tensor_tensor(V[:, :, :], V[:, :, :], X[:, :, :], ALU.add))
            ln_dve(dve, link, s_rq, s_sd, V, X)

        dve_stage(post0, rows=(I["L0_gnn_out_b"],), n_ln=1)

        node_mm(X, [(w_p[:, :], Y, ACT.Copy, False)])

        def deg1(dve, link):
            affine(dve, link, Y, None, 0)
            dve.tensor_scalar(red[:, :], degd[:, :], 1.0, None, ALU.add).then_inc(s_rq.h, 1)
            s_rq.past(1)
            s_sd.past(1)
            dve.wait_ge(s_sd.h, s_sd.base)
            link(dve.reciprocal(dinv[:, :], red2[:, :]))

        dve_stage(deg1, rows=(I["L1_gnn_bp"],), n_ln=1)
        act_stage(lambda act, link: link(nc.scalar.activation(Y[:, :, :], Y[:, :, :], ACT.Gelu)))
        for k in range(3):
            node_mm(Y, [(w_g[k][:, :], Z, ACT.Copy, False)])
            dve_stage(lambda dve, link: link(dve.tensor_tensor(Z[:, :, :], Z[:, :, :], bc_last(dinv[:, :], D),
                                                               ALU.mult)))
            load_store([(nodes(h_t), Z[:, :, :])])
            spmm(h_t, src_i, dstf, dsc_i, False, acc[k])
            sum_tables(acc[k], Y, (V,))

            def conv(dve, link):
                link(dve.tensor_tensor(Y[:, :, :], Y[:, :, :], Z[:, :, :], ALU.add))
                link(dve.tensor_tensor(Y[:, :, :], Y[:, :, :], bc_last(dinv[:, :], D), ALU.mult))
                affine(dve, link, Y, None, 0)

            dve_stage(conv, rows=(I[f"L1_gnn_b{k}"],))

        def post1(dve, link):
            link(dve.tensor_tensor(Y[:, :, :], Y[:, :, :], X[:, :, :], ALU.add))
            ln_dve(dve, link, s_rq, s_sd, Y, X)

        dve_stage(post1, n_ln=1)

        load_store([(nodes(h_t), X[:, :, :])])
        spmm(h_t, src_i, dstf, dsc_i, True, acc[3])
        sum_tables(acc[3], Y, (Z, V))

        def pre2(dve, link):
            link(dve.tensor_tensor(Z[:, :, :], Y[:, :, :], X[:, :, :], ALU.mult))
            link(dve.tensor_tensor(Y[:, :, :], Y[:, :, :], X[:, :, :], ALU.add))

        dve_stage(pre2)
        node_mm(Y, [(w_n1[:, :], V, ACT.Copy, False)])
        node_mm(Z, [(w_n2[:, :], Y, ACT.Copy, False)])

        def post2(dve, link):
            link(dve.tensor_tensor(V[:, :, :], V[:, :, :], Y[:, :, :], ALU.add))
            affine(dve, link, V, None, 0)
            affine(dve, link, V, None, 1)
            link(dve.scalar_tensor_tensor(V[:, :, :], V[:, :, :], 0.2, V[:, :, :], ALU.mult, ALU.max))
            link(dve.tensor_tensor(V[:, :, :], V[:, :, :], X[:, :, :], ALU.add))
            ln_dve(dve, link, s_rq, s_sd, V, X)

        dve_stage(post2, rows=(I["L2_gnn_b1"], I["L2_gnn_b2"]), n_ln=1)

        rel_v = rel_t.rearrange("(p b t) d -> p b (t d)", b=NB, t=NT)
        node_mm(X, [(w_rel[:, k * 512:(k + 1) * 512], rel_v[:, :, k * 512:(k + 1) * 512], ACT.Copy, True)
                    for k in range(NT * D // 512)])
        spmm(rel_t, rel_i, srcf, ssc_i, True, acc[4])
        sum_tables(acc[4], Y, (Z, V))
        node_mm(X, [(w_self[:, :], V, ACT.Copy, False)])

        def post3(dve, link):
            link(dve.tensor_scalar(degs[:, :], degs[:, :], 1e-12, None, ALU.max))
            link(dve.reciprocal(degs[:, :], degs[:, :]))
            link(dve.tensor_tensor(Y[:, :, :], Y[:, :, :], bc_last(degs[:, :], D), ALU.mult))
            ln_dve(dve, link, s_rq, s_sd, Y, Z)
            affine(dve, link, Z, 0, 1)
            affine(dve, link, Z, None, 2)
            link(dve.tensor_tensor(Z[:, :, :], Z[:, :, :], V[:, :, :], ALU.add))
            link(dve.tensor_tensor(Z[:, :, :], Z[:, :, :], X[:, :, :], ALU.add))
            ln_dve(dve, link, s_rq, s_sd, Z, Y)

        dve_stage(post3, rows=(I["L3_gnn_ln_gamma"], I["L3_gnn_ln_beta"], I["L3_gnn_bias"]), n_ln=2)
        load_store([(out.rearrange("(p b) d -> p b d", b=NB), Y[0:PU, :, :])])
    return nc


_INS = ["x", "src", "dst", "edge_attr_64", "edge_type_16", "edge_weight", "L0_gnn_k_w", "L0_gnn_q_w", "L0_gnn_v_w",
        "L0_gnn_wk1_w", "L0_gnn_wk1_b", "L0_gnn_wk2_w", "L0_gnn_wk2_b", "L0_gnn_wkl_w", "L0_gnn_wkl_b",
        "L0_gnn_wv1_w", "L0_gnn_wv1_b", "L0_gnn_wv2_w", "L0_gnn_wv2_b", "L0_gnn_wvl_w", "L0_gnn_wvl_b",
        "L0_gnn_out_w", "L0_gnn_out_b", "L0_gnn_ln1_g", "L0_gnn_ln1_b", "L0_gnn_ln2_g", "L0_gnn_ln2_b",
        "L1_gnn_Wp", "L1_gnn_bp", "L1_gnn_W0", "L1_gnn_b0", "L1_gnn_W1", "L1_gnn_b1", "L1_gnn_W2", "L1_gnn_b2",
        "L2_gnn_W1", "L2_gnn_b1", "L2_gnn_W2", "L2_gnn_b2", "L3_gnn_weight", "L3_gnn_alpha", "L3_gnn_bias",
        "L3_gnn_w_self", "L3_gnn_ln_gamma", "L3_gnn_ln_beta"]


def kernel(**inputs):
    import numpy as _np
    import concourse.bacc as _bacc
    from concourse import mybir as _mybir
    from concourse.bass_utils import run_bass_kernel_spmd as _run

    nc = _bacc.Bacc("TRN2", target_bir_lowering=False, num_devices=1)
    arrays, aps = {}, {}
    for name in _INS:
        a = _np.ascontiguousarray(inputs[name])
        arrays[f"in_{name}_dram"] = a
        aps[name] = nc.dram_tensor(f"in_{name}_dram", a.shape, _mybir.dt.from_np(a.dtype), kind="ExternalInput").ap()
    out = nc.dram_tensor("out_dram", inputs["x"].shape, _mybir.dt.float32, kind="ExternalOutput").ap()
    build(nc, aps, out)
    r = _run(nc, [arrays], core_ids=[0])
    return r.results[0]["out_dram"]
```

```python
from contextlib import ExitStack

import numpy as np
import concourse.bass as bass
from concourse import mybir

F32 = mybir.dt.float32
I32 = mybir.dt.int32
BF16 = mybir.dt.bfloat16
U32 = mybir.dt.uint32
ALU = mybir.AluOpType
ACT = mybir.ActivationFunctionType
AX = mybir.AxisListType.X

P = 128
LN_EPS = 1e-5
BIG = 1.0e38
HALF = 4
SLOTS = 2 * HALF
GB = 5


AHEAD = 8
RING_SEMS = (
    "diag_ready", "keys_broadcast", "onehots_ready", "onehots_transposed",
    "transposes_kept", "counts_updated", "counts_kept", "lookups_ready",
    "ranks_ready", "positions_ready", "chain_steps_done", "equality_ready",
    "combined", "staged", "attr_transposed", "attr_copied",
    "hidden_sums", "relu_ready", "log_ready", "hidden_ready",
    "edge_weights_ready", "products_made", "queries_ready", 
    "exponentials_ready",
    "message_rows_ready", "products_copied",
)


class Sem:

    def __init__(self, handle):
        self.h = handle
        self.base = 0

    def at(self, v):
        return self.base + v

    def past(self, v):
        self.base += v


def build(nc, I, out):
    N, D = I["x"].shape
    E, EC = I["edge_attr_64"].shape
    NH, KH, _ = I["L0_gnn_k_w"].shape
    NT, NBAS = I["L3_gnn_alpha"].shape
    PU = 125
    NB = N // PU
    assert PU * NB == N and NB % GB == 0
    NP = P * NB
    assert N < NP
    STRIDE = (E // P // 10) * 10
    T = E - (P - 1) * STRIDE
    assert STRIDE <= T and T % SLOTS == 0
    TS = -(-(T + NB) // P) * P
    ITS = TS // SLOTS
    ITM = -(-(E + N) // (P * SLOTS))
    TI = TS + HALF
    NR = P * TS
    QW = D + NH

    top = ExitStack()
    names = [0]
    n_loads = []

    def sb(ctx, name, shape, dt=F32):
        names[0] += 1
        return ctx.enter_context(nc.sbuf_tensor(f"{name}_{names[0]}", shape, dt))

    def ps(ctx, name, shape, dt=F32):
        names[0] += 1
        return ctx.enter_context(nc.psum_tensor(f"{name}_{names[0]}", shape, dt))

    def sem(name):
        return Sem(top.enter_context(nc.semaphore(name)))

    def dram(name, shape):
        return nc.dram_tensor(name, shape, F32, kind="Internal").ap()

    def linker(eng, s):
        def link(ins):
            s.past(1)
            ins.then_inc(s.h, 1)
            eng.wait_ge(s.h, s.base)
        return link

    kv_t = dram("kv_t", (NP, 2 * D))
    q_t = dram("q_t", (NP, QW))
    h_t = dram("h_t", (NP, D))
    rel_t = dram("rel_t", (NP * NT, D))
    u_d = dram("u_d", (P, TS * D))
    rec_d = dram("rec_d", (NR, 4))
    RW = 4 + EC
    rec_s = dram("rec_s", (NR, RW))

    with top:
        ring = {name: sem(name) for name in RING_SEMS}
        s_v = sem("dve_chain")
        s_a = sem("act_chain")
        s_p = sem("pool_chain")
        s_t = sem("pe_chain")
        s_ld = sem("loads_landed")
        s_st = sem("stores_landed")
        s_x1 = sem("stage_signal_1")
        s_x2 = sem("stage_signal_2")
        s_x3 = sem("stage_signal_3")
        s_x4 = sem("stage_signal_4")

        ioh = sb(top, "ioh", [P, P])
        ident = sb(top, "ident", [P, P])
        ones = sb(top, "ones", [P, P])
        above = sb(top, "above", [P, 1])
        epsc = sb(top, "epsc", [P, 1])
        halfc = sb(top, "halfc", [P, 1])
        X = sb(top, "X", [P, NB, D])
        gdst_i = sb(top, "gdst_i", [P, TI], I32)
        realS = sb(top, "realS", [P, TS])
        keyT = sb(top, "keyT", [P, TS // P, P])
        degd = sb(top, "degd", [P, NB])
        scount = sb(top, "scount", [P, NB])
        gsrc_i, grel_i = sb(top, "gsrc_i", [P, TI], I32), sb(top, "grel_i", [P, TI], I32)
        wD, wS = sb(top, "wD", [P, TS]), sb(top, "wS", [P, TS])
        locD, locS = sb(top, "locD", [P, TS]), sb(top, "locS", [P, TS])
        firstD, firstS = sb(top, "firstD", [1, TS], I32), sb(top, "firstS", [1, TS], I32)
        degs = sb(top, "degs", [P, NB])
        dinv = sb(top, "dinv", [P, NB])
        red = sb(top, "red", [P, NB])
        red2 = sb(top, "red2", [P, NB])
        rowb = sb(top, "rowb", [P, 4, D])

        def bc_mid(ap2, n):
            return ap2.unsqueeze(1).to_broadcast([ap2.shape[0], n, ap2.shape[1]])

        def bc_last(ap2, n):
            return ap2.unsqueeze(2).to_broadcast([ap2.shape[0], ap2.shape[1], n])

        def over(ap1, width):
            return bass.AP(ap1.tensor, 0, [[STRIDE * width, P], [1, T * width]])

        raw = ExitStack()
        srcf, dstf = sb(raw, "srcf", [P, TI]), sb(raw, "dstf", [P, TI])
        wf, relf = sb(raw, "wf", [P, TI]), sb(raw, "relf", [P, TI])
        real = sb(raw, "real", [P, TI])

        with ExitStack() as c:
            isrc = sb(c, "isrc", [P, T], I32)
            idst = sb(c, "idst", [P, T], I32)
            ityp = sb(c, "ityp", [P, T], I32)
            last = sb(c, "last", [P, 1])
            nlast = sb(c, "nlast", [P, 1])
            ptmp = sb(c, "ptmp", [P, 1])
            own = sb(c, "own", [P, NB])
            block = c.enter_context(nc.Block())

            @block.sync
            def _(sp):
                for r in ring.values():
                    sp.sem_inc(r.h, AHEAD)
                    r.past(AHEAD)
                sp.dma_start(isrc[:, :], over(I["src"], 1)).then_inc(s_ld.h, 16)
                sp.dma_start(idst[:, :], over(I["dst"], 1)).then_inc(s_ld.h, 16)
                sp.dma_start(ityp[:, :], over(I["edge_type_16"], 1)).then_inc(s_ld.h, 16)
                sp.dma_start(wf[:, 0:T], over(I["edge_weight"], 1)).then_inc(s_ld.h, 16)
                sp.wait_ge(s_x1.h, 1)
                sp.dma_start(X[0:PU, :, :], I["x"].rearrange("(p b) d -> p b d", b=NB)).then_inc(s_ld.h, 16)
                sp.wait_ge(s_ld.h, 80)

            @block.gpsimd
            def _(pool):
                link = linker(pool, s_p)
                link(nc.gpsimd.memset(ident[:, :], 0.0))
                link(nc.gpsimd.affine_select(out=ident[:, :], in_=ident[:, :], compare_op=ALU.not_equal, fill=1.0,
                                             base=0, pattern=[[-1, P]], channel_multiplier=1))
                link(nc.gpsimd.iota(own[:, :], [[1, NB]], base=0, channel_multiplier=NB,
                                    allow_small_or_imprecise_dtypes=True))
                link(nc.gpsimd.iota(ioh[:, :], [[1, P]], base=0, channel_multiplier=0,
                                    allow_small_or_imprecise_dtypes=True))
                link(nc.gpsimd.iota(above[:, :], [[0, 1]], base=N, channel_multiplier=1,
                                    allow_small_or_imprecise_dtypes=True))

            @block.vector
            def _(dve):
                link = linker(dve, s_v)
                dve.memset(ones[:, :], 1.0)
                dve.memset(epsc[:, :], LN_EPS)
                dve.memset(halfc[:, :], 0.5)
                dve.memset(wf[:, T:TI], 0.0)
                dve.memset(X[:, :, :], 0.0).then_inc(s_x1.h, 1)
                dve.wait_ge(s_ld.h, 80)
                dve.wait_ge(s_p.h, 5)
                link(dve.tensor_scalar(own[:, :], own[:, :], float(N), None, ALU.min))
                link(dve.tensor_scalar(last[:, :], above[:, :], float(N + P - 1), None, ALU.is_equal))
                link(dve.tensor_scalar(nlast[:, :], last[:, :], -float(N), float(N), ALU.mult, ALU.add))
                for raw_i, keyf in ((isrc, srcf), (idst, dstf)):
                    link(dve.tensor_copy(keyf[:, 0:T], raw_i[:, :]))
                    link(dve.tensor_scalar(keyf[:, STRIDE:T], keyf[:, STRIDE:T], last[:, 0:1], nlast[:, 0:1],
                                           ALU.mult, ALU.add))
                    link(dve.memset(keyf[:, T:TI], float(N)))
                    link(dve.tensor_copy(keyf[:, T:T + NB], own[:, :]))
                link(dve.tensor_scalar(wf[:, STRIDE:T], wf[:, STRIDE:T], last[:, 0:1], None, ALU.mult))
                link(dve.memset(real[:, :], 0.0))
                link(dve.memset(real[:, 0:STRIDE], 1.0))
                link(dve.tensor_scalar(real[:, STRIDE:T], real[:, STRIDE:T], last[:, 0:1], None, ALU.add))
                link(dve.memset(relf[:, :], 0.0))
                link(dve.tensor_copy(relf[:, 0:T], ityp[:, :]))
                link(dve.scalar_tensor_tensor(relf[:, :], dstf[:, :], float(NT), relf[:, :], ALU.mult, ALU.add))

            s_ld.past(80)
            s_x1.past(1)

        s_diag = ring["diag_ready"]
        s_bc = ring["keys_broadcast"]
        s_oh = ring["onehots_ready"]
        s_ohT = ring["onehots_transposed"]
        s_ohc = ring["transposes_kept"]
        s_upd = ring["counts_updated"]
        s_cur = ring["counts_kept"]
        s_look = ring["lookups_ready"]
        s_bef = ring["ranks_ready"]
        s_pos = ring["positions_ready"]
        g_landed = [sem(f"rows{s}_landed") for s in range(SLOTS)]
        g2_landed = [sem(f"rows_b{s}_landed") for s in range(SLOTS)]
        scattered = [sem(f"sums{s}_scattered") for s in range(SLOTS)]
        s_went = sem("pool_went_on")
        bound = {}

        def carry():
            nc.gpsimd.sem_inc(s_went.h, 1)

        def set_bounds(pool, *tables):
            bound.clear()
            for t in tables:
                if t.shape[0] not in bound:
                    bound[t.shape[0]] = pool.to_reg(t.shape[0] - 1)

        def gather(dst, table, idx, s):
            nc.gpsimd.indirect_dma_start(dst, None, table, bass.IndirectOffsetOnAxis(ap=idx.bitcast(U32), axis=0),
                                         bounds_check=bound[table.shape[0]], oob_is_err=True).then_inc(s.h, 16)

        def scatter(table, idx, src, s, add=True):
            nc.gpsimd.indirect_dma_start(table, bass.IndirectOffsetOnAxis(ap=idx.bitcast(U32), axis=0), src, None,
                                         bounds_check=bound[table.shape[0]], oob_is_err=True,
                                         **({"compute_op": ALU.add} if add else {})).then_inc(s.h, 16)

        def digits(dve, link, keyf, hi, lo, tf, ti):
            link(dve.tensor_scalar(tf[:, :], keyf[:, :], 1.0 / NB, None, ALU.mult))
            link(dve.tensor_copy(ti[:, :], tf[:, :]))
            link(dve.tensor_copy(hi[:, :], ti[:, :]))
            link(dve.scalar_tensor_tensor(lo[:, :], hi[:, :], -float(NB), keyf[:, :], ALU.mult, ALU.add))
            link(dve.tensor_scalar(tf[:, :], lo[:, :], 0.0, None, ALU.is_lt))
            link(dve.tensor_tensor(hi[:, :], hi[:, :], tf[:, :], ALU.subtract))
            link(dve.scalar_tensor_tensor(lo[:, :], tf[:, :], float(NB), lo[:, :], ALU.mult, ALU.add))
            link(dve.tensor_scalar(tf[:, :], lo[:, :], float(NB), None, ALU.is_ge))
            link(dve.tensor_tensor(hi[:, :], hi[:, :], tf[:, :], ALU.add))
            link(dve.scalar_tensor_tensor(lo[:, :], tf[:, :], -float(NB), lo[:, :], ALU.mult, ALU.add))

        def sort_stage(keyf, fields, rec, cnt, wsum, attributes=None):
            with ExitStack() as c:
                ahead = sb(c, "ahead", [P, HALF, P])
                tri = ahead[:, HALF - 1, :]
                triu = sb(c, "triu", [P, P])
                hi, lo = sb(c, "hi", [P, TI]), sb(c, "lo", [P, TI])
                ti, tf = sb(c, "ti", [P, TI], I32), sb(c, "tf", [P, TI])
                before = sb(c, "before", [P, HALF])
                prev = sb(c, "prev", [P, HALF])
                recs = sb(c, "recs", [P, TS, 4])
                diag = sb(c, "diag", [P, 2, HALF, P])
                same = sb(c, "same", [P, HALF * (HALF + 1) // 2 * P])
                looked = sb(c, "looked", [P, HALF, NB])
                ohhb, ohlb = sb(c, "ohhb", [P, 2, HALF, P], BF16), sb(c, "ohlb", [P, 2, HALF, NB], BF16)
                identb = sb(c, "identb", [P, P], BF16)
                parts = 4 if wsum is not None else 1
                ohw = sb(c, "ohw", [P, 2, parts, HALF, NB], BF16)
                wpart = [sb(c, f"wpart{k}", [P, TI if wsum is not None else 1], BF16) for k in range(3)]
                rest = sb(c, "rest", [P, TI if wsum is not None else 1])
                ohT = sb(c, "ohT", [P, 2, HALF, P])
                slot = sb(c, "slot", [P, 2, HALF, rec.shape[1]])
                cur = sb(c, "cur", [P, 2, NB])
                pre, pre2 = sb(c, "pre", [P, NB]), sb(c, "pre2", [P, NB])
                tot, posf = sb(c, "tot", [P, 1]), sb(c, "posf", [P, HALF])
                pos_i = sb(c, "pos_i", [P, 2, HALF], I32)
                zero = sb(c, "zero", [P, 4 * NB], BF16)
                pcnt, pcur, pbase = ps(c, "pcnt", [P, 512]), ps(c, "pcur", [P, 512]), ps(c, "pbase", [P, 512])
                pbc, poT = ps(c, "pbc", [P, 2, HALF, P]), ps(c, "poT", [P, 2 * HALF, P], BF16)
                plk = ps(c, "plk", [P, 2, HALF, P])

                def onehots(c0, high, low):
                    nc.vector.tensor_tensor(high, bc_mid(ioh[:, :], HALF), bc_last(hi[:, bass.ds(c0, HALF)], P),
                                            ALU.is_equal)
                    return nc.vector.tensor_tensor(low, bc_mid(ioh[:, 0:NB], HALF),
                                                   bc_last(lo[:, bass.ds(c0, HALF)], NB), ALU.is_equal)

                with nc.Block() as block:
                    @block.gpsimd
                    def _(pool):
                        link = linker(pool, s_p)
                        link(nc.gpsimd.memset(ahead[:, :, :], 1.0))
                        link(nc.gpsimd.memset(triu[:, :], 1.0))
                        link(nc.gpsimd.affine_select(out=tri, in_=tri, compare_op=ALU.is_gt, fill=0.0,
                                                     base=0, pattern=[[-1, P]], channel_multiplier=1))
                        link(nc.gpsimd.affine_select(out=triu[:, :], in_=triu[:, :], compare_op=ALU.is_gt, fill=0.0,
                                                     base=0, pattern=[[1, P]], channel_multiplier=-1))

                    @block.vector
                    def _(dve):
                        link = linker(dve, s_v)
                        dve.memset(zero[:, :], 0.0).then_inc(s_x4.h, 1)
                        dve.tensor_copy(identb[:, :], ident[:, :])
                        for k, f in enumerate(fields):
                            dve.tensor_copy(recs[:, :, k], f[:, 0:TS])
                        digits(dve, link, keyf, hi, lo, tf, ti)
                        if wsum is not None:
                            link(dve.tensor_copy(rest[:, :], wf[:, :]))
                            for k in range(3):
                                link(dve.tensor_copy(wpart[k][:, :], rest[:, :]))
                                link(dve.tensor_tensor(rest[:, :], rest[:, :], wpart[k][:, :], ALU.subtract))
                        with dve.Fori(0, ITS) as i:
                            for h in range(2):
                                c0 = i * SLOTS + h * HALF
                                dve.wait_ge(s_upd.h, s_upd.at(i * 2 + h - 1))
                                ins = onehots(c0, ohhb[:, h, :, :], ohw[:, h, 0, :, :])
                                if wsum is not None:
                                    ins.then_inc(s_cmp.h, 1)
                                    dve.wait_ge(s_cmp.h, s_cmp.at(i * 2 + h + 1))
                                    for k in range(3):
                                        ins = dve.tensor_tensor(ohw[:, h, 1 + k, :, :], ohw[:, h, 0, :, :],
                                                                bc_last(wpart[k][:, bass.ds(c0, HALF)], NB), ALU.mult)
                                ins.then_inc(s_oh.h, 1)
                        dve.wait_ge(s_t.h, s_t.at(1))
                        link(dve.tensor_copy(cnt[:, :], pcnt[:, 0:NB]))
                        if wsum is not None:
                            link(dve.tensor_copy(wsum[:, :], pcnt[:, NB:2 * NB]))
                            for k in (2, 3):
                                link(dve.tensor_tensor(wsum[:, :], wsum[:, :], pcnt[:, k * NB:(k + 1) * NB], ALU.add))
                        dve.tensor_reduce(tot[:, :], cnt[:, :], AX, ALU.add).then_inc(s_x1.h, 1)
                        link(dve.tensor_copy(pre[:, :], cnt[:, :]))
                        a, b, step = pre, pre2, 1
                        while step < NB:
                            link(dve.tensor_copy(b[:, 0:step], a[:, 0:step]))
                            link(dve.tensor_tensor(b[:, step:NB], a[:, step:NB], a[:, 0:NB - step], ALU.add))
                            a, b, step = b, a, 2 * step
                        link(dve.tensor_tensor(a[:, :], a[:, :], cnt[:, :], ALU.subtract))
                        dve.wait_ge(s_t.h, s_t.at(2))
                        link(dve.tensor_copy(tot[:, :], pbase[:, 0:1]))
                        link(dve.tensor_scalar(cur[:, 1, :], a[:, :], tot[:, 0:1], None, ALU.add))

                    @block.tensor
                    def _(pe):
                        pe.wait_ge(s_x4.h, s_x4.at(1))
                        nc.tensor.matmul(pcnt[:, 0:parts * NB], zero[:, 0:P], zero[:, 0:parts * NB], start=True, stop=False,
                                         skip_group_check=True)
                        with pe.Fori(0, ITS) as i:
                            for h in range(2):
                                pe.wait_ge(s_oh.h, s_oh.at(i * 2 + h + 1))
                                for u in range(HALF):
                                    ins = nc.tensor.matmul(pcnt[:, 0:parts * NB], ohhb[:, h, u, :],
                                                           ohw[:, h, :, u, :], start=False, stop=False,
                                                           skip_group_check=True)
                                ins.then_inc(s_upd.h, 1)
                        nc.tensor.matmul(pcnt[:, 0:parts * NB], zero[:, 0:P], zero[:, 0:parts * NB], start=False, stop=True,
                                         skip_group_check=True).then_inc(s_t.h, 1)
                        pe.wait_ge(s_x1.h, s_x1.at(1))
                        pe.wait_ge(s_p.h, s_p.base)
                        nc.tensor.matmul(pbase[:, 0:1], triu[:, :], tot[:, :], start=True,
                                         stop=True).then_inc(s_t.h, 1)

                    s_x1.past(1)
                    s_x4.past(1)
                    s_t.past(2)
                    s_oh.past(2 * ITS)
                    s_upd.past(2 * ITS)
                    s_cmp.past(2 * ITS if wsum is not None else 0)

                with nc.Block() as block:
                    @block.vector
                    def _(dve):
                        def keys_of(n, h, c0):
                            dve.wait_ge(s_upd.h, s_upd.at(n - 1))
                            dve.wait_ge(s_bef.h, s_bef.at(n - 1))
                            onehots(c0, ohhb[:, h, :, :], ohlb[:, h, :, :]).then_inc(s_oh.h, 1)
                            dve.wait_ge(s_bc.h, s_bc.at(n - 1))
                            dve.tensor_tensor(diag[:, h, :, :], bc_mid(ident[:, :], HALF),
                                              bc_last(keyf[:, bass.ds(c0, HALF)], P), ALU.mult).then_inc(s_diag.h, 1)

                        keys_of(0, 0, 0)
                        with dve.Fori(0, ITS) as i:
                            for h in range(2):
                                n = i * 2 + h
                                c0 = i * SLOTS + h * HALF
                                keys_of(n + 1, 1 - h, c0 + HALF)
                                dve.wait_ge(s_bc.h, s_bc.at(n + 1))
                                for u in range(HALF):
                                    a, w = u * (u + 1) // 2 * P, (u + 1) * P
                                    dve.scalar_tensor_tensor(
                                        same[:, a:a + w], pbc[:, h, :, :].rearrange("p u q -> p (u q)")[:, 0:w],
                                        keyf[:, bass.ds(c0 + u, 1)],
                                        ahead[:, :, :].rearrange("p u q -> p (u q)")[:, HALF * P - w:HALF * P],
                                        ALU.is_equal, ALU.mult, accum_out=before[:, u:u + 1])
                                dve.wait_ge(s_look.h, s_look.at(n + 1))
                                dve.tensor_tensor(looked[:, :, :], plk[:, h, :, 0:NB], ohlb[:, h, :, :],
                                                  ALU.mult).then_inc(s_cmp.h, 1)
                                dve.wait_ge(s_cmp.h, s_cmp.at(n * 2 + 1))
                                dve.tensor_reduce(prev[:, :], looked[:, :, :], AX, ALU.add).then_inc(s_cmp.h, 1)
                                dve.wait_ge(s_cmp.h, s_cmp.at(n * 2 + 2))
                                dve.tensor_tensor(posf[:, :], before[:, :], prev[:, :], ALU.add).then_inc(s_bef.h, 1)
                                dve.wait_ge(s_bef.h, s_bef.at(n + 1))
                                for u in range(HALF):
                                    s = scattered[h * HALF + u]
                                    dve.wait_ge(s.h, s.at(16 * i))
                                dve.tensor_copy(pos_i[:, h, :], posf[:, :]).then_inc(s_pos.h, 1)
                                dve.wait_ge(s_pos.h, s_pos.at(n + 1))

                    @block.tensor
                    def _(pe):
                        def keys_of(n, h):
                            pe.wait_ge(s_oh.h, s_oh.at(n + 1))
                            pe.wait_ge(s_ohc.h, s_ohc.at(n))
                            for u in range(HALF):
                                ins = nc.tensor.transpose(poT[:, u, :], ohhb[:, h, u, :], identb[:, :])
                            ins.then_inc(s_ohT.h, 1)
                            pe.wait_ge(s_diag.h, s_diag.at(n + 1))
                            pe.wait_ge(s_bef.h, s_bef.at(n - 1))
                            nc.tensor.matmul(pbc[:, h, :, :].rearrange("p u q -> p (u q)"), ones[:, :],
                                             diag[:, h, :, :].rearrange("p u q -> p (u q)"), start=True,
                                             stop=True).then_inc(s_bc.h, 1)

                        nc.tensor.matmul(pcur[:, 0:NB], ident[:, :], cur[:, 1, :], start=True, stop=False,
                                         skip_group_check=True)
                        keys_of(0, 0)
                        with pe.Fori(0, ITS) as i:
                            for h in range(2):
                                n = i * 2 + h
                                pe.wait_ge(s_ohc.h, s_ohc.at(n + 1))
                                pe.wait_ge(s_cur.h, s_cur.at(n))
                                pe.wait_ge(s_bef.h, s_bef.at(n - 1))
                                for u in range(HALF):
                                    ins = nc.tensor.matmul(plk[:, h, u, 0:NB], ohT[:, h, u, :], cur[:, 1 - h, :],
                                                           start=True, stop=True)
                                ins.then_inc(s_look.h, 1)
                                for u in range(HALF):
                                    ins = nc.tensor.matmul(pcur[:, 0:NB], ohhb[:, h, u, :], ohlb[:, h, u, :],
                                                           start=False, stop=False, skip_group_check=True)
                                ins.then_inc(s_upd.h, 1)
                                keys_of(n + 1, 1 - h)

                    @block.scalar
                    def _(act):
                        def transposes_of(n, h):
                            act.wait_ge(s_ohT.h, s_ohT.at(n + 1))
                            act.wait_ge(s_look.h, s_look.at(n - 1))
                            nc.scalar.activation(ohT[:, h, :, :], poT[:, 0:HALF, :], ACT.Copy).then_inc(s_ohc.h, 1)

                        act.preload_act_table(ACT.Exp)
                        transposes_of(0, 0)
                        with act.Fori(0, ITS) as i:
                            for h in range(2):
                                n = i * 2 + h
                                act.wait_ge(s_upd.h, s_upd.at(n + 1))
                                act.wait_ge(s_look.h, s_look.at(n))
                                nc.scalar.activation(cur[:, h, :], pcur[:, 0:NB], ACT.Copy).then_inc(s_cur.h, 1)
                                transposes_of(n + 1, 1 - h)

                    @block.sync
                    def _(sp):
                        if attributes is None:
                            return
                        for a, b in ((0, T // SLOTS), (T // SLOTS, ITS)):
                            with sp.Fori(a, b) as i:
                                for h in range(2):
                                    for u in range(HALF):
                                        s = scattered[h * HALF + u]
                                        sp.wait_ge(s.h, s.at(16 * i))
                                    sp.dma_start(slot[:, h, :, 4:RW],
                                                 attributes[:, bass.ds((i * SLOTS + h * HALF - a * SLOTS) * EC,
                                                                       HALF * EC)]
                                                 .rearrange("p (u d) -> p u d", d=EC)).then_inc(slot_landed[h].h, 16)

                    @block.gpsimd
                    def _(pool):
                        set_bounds(pool, rec)
                        with pool.Fori(0, ITS) as i:
                            for h in range(2):
                                c0 = i * SLOTS + h * HALF
                                pool.wait_ge(s_pos.h, s_pos.at(i * 2 + h + 1))
                                pool.tensor_copy(slot[:, h, :, 0:4], recs[:, bass.ds(c0, HALF), :]).then_inc(s_p.h, 1)
                                pool.wait_ge(s_p.h, s_p.at(i * 2 + h + 1))
                                if attributes is not None:
                                    pool.wait_ge(slot_landed[h].h, slot_landed[h].at(i * 16 + 16))
                                carry()
                                for u in range(HALF):
                                    scatter(rec, pos_i[:, h, u:u + 1], slot[:, h, u, :], scattered[h * HALF + u],
                                            add=False)
                        for s in range(SLOTS):
                            pool.wait_ge(scattered[s].h, scattered[s].at(16 * ITS))

                    for s in (s_diag, s_bc, s_oh, s_ohT, s_ohc):
                        s.past(2 * ITS + 1)
                    for s in (s_bef, s_pos, s_p, s_upd, s_cur, s_look):
                        s.past(2 * ITS)
                    s_cmp.past(4 * ITS)
                    for s in range(SLOTS):
                        scattered[s].past(16 * ITS)
                    if attributes is not None:
                        for h in range(2):
                            slot_landed[h].past(16 * ITS)

        slot_landed = [sem(f"slot{h}_landed") for h in range(2)]
        s_cmp = ring["chain_steps_done"]
        sort_stage(srcf, (relf, wf, srcf, real), rec_s, scount, degs, over(I["edge_attr_64"], EC))
        sort_stage(dstf, (srcf, wf, dstf, real), rec_d, degd, None)
        raw.close()

        def sorted_lists(rec, gidx, weight, local, first, flag=None, keyrows=None):
            NBK, w = TS // P, rec.shape[1]
            outs = [gidx, weight, None] + ([flag] if flag is not None else [])
            nf = len(outs)
            with ExitStack() as c:
                rows = sb(c, "rows", [P, 2, P, w])
                key = sb(c, "key", [P, TS])
                pt = ps(c, "pt", [P, 2, 512])
                pk = ps(c, "pk", [P, 2, 512])
                block = c.enter_context(nc.Block())
                outs[2] = key

                @block.sync
                def _(sp):
                    for k in range(NBK):
                        if k >= 2:
                            sp.wait_ge(s_x1.h, s_x1.at(k - 1))
                        sp.dma_start(rows[:, k % 2, :, :].rearrange("t p f -> t (p f)"),
                                     rec[k * P * P:(k + 1) * P * P, :].rearrange("(t p) f -> t (p f)", p=P))\
                            .then_inc(slot_landed[k % 2].h, 16)

                @block.tensor
                def _(pe):
                    for k in range(NBK):
                        pe.wait_ge(slot_landed[k % 2].h, slot_landed[k % 2].at(16 * (k // 2 + 1)))
                        if k >= 2:
                            pe.wait_ge(s_x1.h, s_x1.at(k - 1))
                        for f in range(nf):
                            ins = nc.tensor.transpose(pt[:, k % 2, f * P:(f + 1) * P], rows[:, k % 2, :, f],
                                                      ident[:, :])
                        ins.then_inc(s_t.h, 1)
                        pe.wait_ge(s_x1.h, s_x1.at(k + 1))
                        nc.tensor.matmul(pk[:, k % 2, 0:P], ones[0:1, :], key[0:1, k * P:(k + 1) * P], start=True,
                                         stop=True).then_inc(s_x2.h, 1)

                @block.vector
                def _(dve):
                    link = linker(dve, s_v)
                    link(dve.memset(gidx[:, :], 0))
                    for k in range(NBK):
                        cols = slice(k * P, (k + 1) * P)
                        dve.wait_ge(s_t.h, s_t.at(k + 1))
                        if keyrows is not None:
                            dve.tensor_copy(keyrows[:, k, :], rows[:, k % 2, :, 2])
                        for f, o in enumerate(outs):
                            ins = dve.tensor_copy(o[:, cols], pt[:, k % 2, f * P:(f + 1) * P])
                        ins.then_inc(s_x1.h, 1)
                        dve.wait_ge(s_x1.h, s_x1.at(k + 1))
                        dve.tensor_copy(first[:, cols], key[0:1, cols])
                        dve.wait_ge(s_x2.h, s_x2.at(k + 1))
                        link(dve.tensor_tensor(local[:, cols], key[:, cols], pk[:, k % 2, 0:P], ALU.subtract))
                    if flag is not None:
                        link(dve.tensor_scalar(gdst_i[:, :], gidx[:, :], NT.bit_length() - 1, None,
                                               ALU.logical_shift_right))

                slot_landed[0].past(16 * ((NBK + 1) // 2))
                slot_landed[1].past(16 * (NBK // 2))
                s_x1.past(NBK)
                s_x2.past(NBK)
                s_t.past(NBK)

        assert NT & (NT - 1) == 0
        sorted_lists(rec_d, gsrc_i, wD, locD, firstD)
        sorted_lists(rec_s, grel_i, wS, locS, firstS, realS, keyT)

        Y = sb(top, "Y", [P, NB, D])
        Z = sb(top, "Z", [P, NB, D])
        V = sb(top, "V", [P, NB, D])

        def ln_dve(dve, link, act_req, act_done, src, dst):
            link(dve.tensor_reduce(red[:, :], src[:, :, :], AX, ALU.add))
            link(dve.tensor_scalar(red[:, :], red[:, :], 1.0 / D, None, ALU.mult))
            link(dve.tensor_tensor(src[:, :, :], src[:, :, :], bc_last(red[:, :], D), ALU.subtract))
            link(dve.tensor_tensor(dst[:, :, :], src[:, :, :], src[:, :, :], ALU.mult))
            link(dve.tensor_reduce(red[:, :], dst[:, :, :], AX, ALU.add))
            dve.tensor_scalar(red[:, :], red[:, :], 1.0 / D, LN_EPS, ALU.mult, ALU.add).then_inc(act_req.h, 1)
            act_req.past(1)
            act_done.past(1)
            dve.wait_ge(act_done.h, act_done.base)
            link(dve.reciprocal(red[:, :], red2[:, :]))
            link(dve.tensor_tensor(dst[:, :, :], src[:, :, :], bc_last(red[:, :], D), ALU.mult))

        def sqrt_act(act, req, done, n):
            for k in range(1, n + 1):
                act.wait_ge(req.h, req.at(k))
                nc.scalar.activation(red2[:, :], red[:, :], ACT.Sqrt).then_inc(done.h, 1)

        s_rq = sem("variance_ready")
        s_sd = sem("root_ready")

        def dve_stage(body, rows=(), n_ln=0, act_extra=None):
            with ExitStack() as c:
                block = c.enter_context(nc.Block())
                nrow = len(rows)

                @block.sync
                def _(sp):
                    for k, r in enumerate(rows):
                        sp.dma_start(rowb[:, k, 0:r.shape[0]], r.unsqueeze(0).to_broadcast([P, r.shape[0]])).then_inc(s_ld.h, 16)

                @block.scalar
                def _(act):
                    sqrt_act(act, s_rq, s_sd, n_ln)

                @block.vector
                def _(dve):
                    link = linker(dve, s_v)
                    if nrow:
                        dve.wait_ge(s_ld.h, s_ld.at(16 * nrow))
                    body(dve, link)

                s_ld.past(16 * nrow)

        s_blk = sem("blocks_copied")
        s_tr = sem("blocks_transposed")
        s_trc = sem("transposes_copied")
        s_mm = sem("products_ready")
        s_ev = ring["products_copied"]

        def node_mm(src, weights):
            steps = NB // GB
            with ExitStack() as c:
                xb = sb(c, "xb", [P, GB, D])
                xT = sb(c, "xT", [P, GB, P])
                width = max(w[0].shape[1] for w in weights)
                stored = weights[0][3]
                nw = len(weights)
                assert all(w[3] == stored for w in weights) and (not stored or nw % 2 == 0)
                stage = sb(c, "stage", [P, 2, GB, width if stored else 1])
                pT = ps(c, "pT", [P, 2, 4, P])
                pO = ps(c, "pO", [P, GB, 512])
                block = c.enter_context(nc.Block())

                @block.vector
                def _(dve):
                    with dve.Fori(0, steps) as i:
                        dve.wait_ge(s_tr.h, s_tr.at(i))
                        dve.tensor_copy(xb[:, :, :], src[:, bass.ds(i * GB, GB), :]).then_inc(s_blk.h, 1)

                @block.tensor
                def _(pe):
                    with pe.Fori(0, steps) as i:
                        pe.wait_ge(s_blk.h, s_blk.at(i + 1))
                        pe.wait_ge(s_trc.h, s_trc.at(i))
                        for g in range(GB):
                            ins = nc.tensor.transpose(pT[:, g // 4, g % 4, :], xb[:, g, :], ident[:, :])
                        ins.then_inc(s_tr.h, 1)
                        pe.wait_ge(s_trc.h, s_trc.at(i + 1))
                        for k, (rhs, dst, func, _d) in enumerate(weights):
                            for g in range(GB):
                                q = (i * nw + k) * GB + g
                                pe.wait_ge(s_ev.h, s_ev.at(q + 1 - GB))
                                nc.tensor.matmul(pO[:, g, 0:rhs.shape[1]], xT[:, g, :], rhs, start=True,
                                                 stop=True).then_inc(s_mm.h, 1)

                @block.scalar
                def _(act):
                    with act.Fori(0, steps) as i:
                        act.wait_ge(s_tr.h, s_tr.at(i + 1))
                        act.wait_ge(s_mm.h, s_mm.at(i * nw * GB))
                        nc.scalar.activation(xT[:, 0:4, :], pT[:, 0, :, :], ACT.Copy)
                        nc.scalar.activation(xT[:, 4:5, :], pT[:, 1, 0:1, :], ACT.Copy).then_inc(s_trc.h, 1)
                        for k, (rhs, dst, func, dr) in enumerate(weights):
                            w = rhs.shape[1]
                            if stored:
                                act.wait_ge(slot_landed[k % 2].h, slot_landed[k % 2].at(16 * (i * (nw // 2) + k // 2)))
                            for g in range(GB):
                                act.wait_ge(s_mm.h, s_mm.at((i * nw + k) * GB + g + 1))
                                to = stage[:, k % 2, g, 0:w] if stored else \
                                    dst[:, bass.ds(i * GB + g, 1), :].rearrange("p b d -> p (b d)")
                                nc.scalar.activation(to, pO[:, g, 0:w], func).then_inc(s_ev.h, 1)

                @block.sync
                def _(sp):
                    if not stored:
                        return
                    with sp.Fori(0, steps) as i:
                        for k, (rhs, dst, func, dr) in enumerate(weights):
                            sp.wait_ge(s_ev.h, s_ev.at((i * nw + k + 1) * GB))
                            sp.dma_start(dst[:, bass.ds(i * GB, GB), :], stage[:, k % 2, :, 0:rhs.shape[1]])\
                                .then_inc(slot_landed[k % 2].h, 16)
                    for g in range(2):
                        sp.wait_ge(slot_landed[g].h, slot_landed[g].at(16 * steps * nw // 2))

                for s in (s_blk, s_tr, s_trc):
                    s.past(steps)
                for s in (s_mm, s_ev):
                    s.past(steps * nw * GB)
                if stored:
                    for s in slot_landed:
                        s.past(16 * steps * nw // 2)

        def nodes(t):
            return t.rearrange("(p b) d -> p b d", b=NB)

        def load_store(pairs):
            with ExitStack() as c:
                block = c.enter_context(nc.Block())

                @block.sync
                def _(sp):
                    for a, b in pairs:
                        sp.dma_start(a, b).then_inc(s_st.h, 16)
                    sp.wait_ge(s_st.h, s_st.at(16 * len(pairs)))

                s_st.past(16 * len(pairs))

        s_ix = [sem(f"indices{h}_ready") for h in range(2)]
        s_eq = ring["equality_ready"]
        s_cmb = ring["combined"]
        s_stg = ring["staged"]
        def window_sum(table, gidx, weight, local, first, dst):
            with ExitStack() as c:
                gi = sb(c, "gi", [P, 2, HALF], I32)
                G = sb(c, "G", [P, 2, HALF, D])
                oh = sb(c, "oh", [P, 2, HALF, P])
                resT = V[:, :, :].rearrange("p b d -> p (b d)")
                pw = ps(c, "pw", [P, 2, HALF, P])
                with nc.Block() as block:
                    @block.scalar
                    def _(act):
                        with act.Fori(0, ITM) as i:
                            for h in range(2):
                                for u in range(HALF):
                                    act.wait_ge(g_landed[h * HALF + u].h, g_landed[h * HALF + u].at(i * 16))
                                nc.scalar.activation(gi[:, h, :], gidx[:, bass.ds(i * SLOTS + h * HALF, HALF)],
                                                     ACT.Copy).then_inc(s_ix[h].h, 1)

                    @block.gpsimd
                    def _(pool):
                        set_bounds(pool, table)
                        with pool.Fori(0, ITM) as i:
                            for h in range(2):
                                pool.wait_ge(s_ix[h].h, s_ix[h].at(i + 1))
                                pool.wait_ge(s_cmb.h, s_cmb.at(i * 2 + h - 1))
                                carry()
                                for u in range(HALF):
                                    gather(G[:, h, u, :], table, gi[:, h, u:u + 1], g_landed[h * HALF + u])

                    @block.tensor
                    def _(pe):
                        with pe.Fori(0, ITM) as i:
                            for h in range(2):
                                pe.wait_ge(s_eq.h, s_eq.at(i * 2 + h + 1))
                                pe.wait_ge(s_stg.h, s_stg.at((i * 2 + h - 1) * HALF))
                                for u in range(HALF):
                                    pe.wait_ge(g_landed[h * HALF + u].h, g_landed[h * HALF + u].at(i * 16 + 16))
                                    ins = nc.tensor.matmul(pw[:, h, u, :], G[:, h, u, :], oh[:, h, u, :],
                                                           start=True, stop=True)
                                ins.then_inc(s_cmb.h, 1)

                    @block.vector
                    def _(dve):
                        link = linker(dve, s_v)
                        link(dve.memset(resT[:, :], 0.0))

                        def onehots(c0, h):
                            for u in range(HALF):
                                col = bass.ds(c0 + u, 1)
                                if weight is None:
                                    ins = dve.tensor_scalar(oh[:, h, u, :], ioh[:, :], local[:, col], None,
                                                            ALU.is_equal)
                                else:
                                    ins = dve.tensor_scalar(oh[:, h, u, :], ioh[:, :], local[:, col],
                                                            weight[:, col], ALU.is_equal, ALU.mult)
                            ins.then_inc(s_eq.h, 1)

                        with dve.Fori(0, ITM) as i:
                            for h in range(2):
                                dve.wait_ge(s_cmb.h, s_cmb.at(i * 2 + h - 1))
                                onehots(i * SLOTS + h * HALF, h)
                            for h in range(2):
                                n = i * 2 + h
                                _, keys = nc.values_load_multi_w_load_instructions(
                                    first[0:1, bass.ds(i * SLOTS + h * HALF, HALF)], engines=(mybir.EngineType.DVE,),
                                    min_val=0, max_val=N)
                                dve.wait_ge(s_cmb.h, s_cmb.at(n + 1))
                                for u, k in enumerate(keys):
                                    dve.wait_ge(s_stg.h, s_stg.at(n * HALF + u))
                                    at_k = resT[:, bass.ds(k, P)]
                                    dve.tensor_tensor(at_k, at_k, pw[:, h, u, :], ALU.add).then_inc(s_stg.h, 1)

                    for s in (s_cmb, s_eq):
                        s.past(2 * ITM)
                    s_stg.past(2 * ITM * HALF)
                    for h in range(2):
                        s_ix[h].past(ITM)
                    for s in range(SLOTS):
                        g_landed[s].past(16 * ITM)
                turn_back(c, resT, dst)

        def turn_back(c, resT, dst):
            steps = NB // GB
            R = resT.shape[0]
            xb = sb(c, "xb", [R, GB, P])
            pT = ps(c, "pT", [P, 2, 4, P])
            with nc.Block() as block:
                @block.vector
                def _(dve):
                    with dve.Fori(0, steps) as i:
                        dve.wait_ge(s_tr.h, s_tr.at(i))
                        dve.tensor_copy(xb[:, :, :],
                                        resT[:, :].rearrange("f (p b) -> f b p", b=NB)[:, bass.ds(i * GB, GB), :])\
                            .then_inc(s_blk.h, 1)

                @block.tensor
                def _(pe):
                    with pe.Fori(0, steps) as i:
                        pe.wait_ge(s_blk.h, s_blk.at(i + 1))
                        pe.wait_ge(s_trc.h, s_trc.at(i))
                        if R < P:
                            pe.sem_inc(s_went.h, 1)
                        for g in range(GB):
                            ins = nc.tensor.transpose(pT[:, g // 4, g % 4, 0:R], xb[:, g, :], ident[0:R, 0:R])
                        ins.then_inc(s_tr.h, 1)

                @block.scalar
                def _(act):
                    with act.Fori(0, steps) as i:
                        act.wait_ge(s_tr.h, s_tr.at(i + 1))
                        nc.scalar.activation(dst[:, bass.ds(i * GB, 4), :], pT[:, 0, :, 0:R], ACT.Copy)
                        nc.scalar.activation(dst[:, bass.ds(i * GB + 4, 1), :], pT[:, 1, 0:1, 0:R],
                                             ACT.Copy).then_inc(s_trc.h, 1)

                for s in (s_blk, s_tr, s_trc):
                    s.past(steps)

        def wt(name, w, dt=F32):
            return sb(top, name, [P, w], dt)

        w_kv, w_q, w_vl, w_out = wt("w_kv", 2 * D), wt("w_q", QW), wt("w_vl", D), wt("w_out", D)
        w_p, w_self = wt("w_p", D), wt("w_self", D)
        w_g = [wt(f"w_g{k}", D) for k in range(3)]
        w_n1, w_n2 = wt("w_n1", D), wt("w_n2", D)
        w_rel = wt("w_rel", NT * D)
        w1 = sb(top, "w1", [2 * EC, 4 * KH])
        b1 = sb(top, "b1", [4 * KH, 1])
        w2 = sb(top, "w2", [4 * KH, 4 * KH])
        b2 = sb(top, "b2", [1, 4 * KH])
        with ExitStack() as c:
            qn, ql = sb(c, "qn", [P, D]), sb(c, "ql", [P, QW])
            nat = [sb(c, f"nat{k}", [P, D]) for k in range(3)]
            wbas = sb(c, "wbas", [P, NBAS, D])
            alf = sb(c, "alf", [P, NT, NBAS])
            wtmp = sb(c, "wtmp", [P, NT, D])
            pw = ps(c, "pw", [P, 4, 512])
            block = c.enter_context(nc.Block())
            n_w = 6 * NH + 26

            @block.vector
            def _(dve):
                link = linker(dve, s_v)
                for t in (w_kv, qn, ql, w_vl):
                    dve.memset(t[:, :], 0.0)
                dve.memset(w1[:, :], 0.0)
                dve.memset(w2[:, :], 0.0).then_inc(s_x1.h, 1)
                dve.wait_ge(s_ld.h, s_ld.at(16 * n_w))
                rel = w_rel[:, :].rearrange("p (t d) -> p t d", t=NT)
                for b in range(NBAS):
                    dst = rel if b == 0 else wtmp[:, :, :]
                    link(dve.tensor_tensor(dst, bc_mid(wbas[:, b, :], NT), bc_last(alf[:, :, b], D), ALU.mult))
                    if b:
                        link(dve.tensor_tensor(rel, rel, wtmp[:, :, :], ALU.add))
                dve.wait_ge(s_t.h, s_t.at(4))
                link(dve.tensor_copy(w_q[:, :], pw[:, 0, 0:QW]))
                for k, t in enumerate((w_out, w_n1, w_n2)):
                    link(dve.tensor_copy(t[:, :], pw[:, 1 + k, 0:D]))

            @block.sync
            def _(sp):
                n = [0]

                def ld(dst, src):
                    n[0] += 1
                    sp.dma_start(dst, src).then_inc(s_ld.h, 16)

                sp.wait_ge(s_x1.h, s_x1.at(1))
                with nc.allow_non_contiguous_dma(reason="small transposed weights"):
                    for h in range(NH):
                        r = slice(h * KH, (h + 1) * KH)
                        ld(w_kv[r, r], I["L0_gnn_k_w"][h].rearrange("k d -> d k"))
                        ld(w_kv[r, D + h * KH:D + (h + 1) * KH], I["L0_gnn_v_w"][h].rearrange("k d -> d k"))
                        ld(qn[r, r], I["L0_gnn_q_w"][h])
                        ld(ql[r, r], I["L0_gnn_wkl_w"])
                        ld(ql[r, D + h:D + h + 1], I["L0_gnn_wkl_b"].unsqueeze(1))
                        ld(w_vl[r, r], I["L0_gnn_wvl_w"].rearrange("k d -> d k"))
                    for j in range(2):
                        e0, k0 = j * EC, j * 2 * KH
                        k1, k2 = k0 + KH, k0 + 2 * KH
                        ld(w1[e0:e0 + EC, k0:k1], I["L0_gnn_wk1_w"].rearrange("k d -> d k"))
                        ld(w1[e0:e0 + EC, k1:k2], I["L0_gnn_wv1_w"].rearrange("k d -> d k"))
                        ld(b1[k0:k1, :], I["L0_gnn_wk1_b"].unsqueeze(1))
                        ld(b1[k1:k2, :], I["L0_gnn_wv1_b"].unsqueeze(1))
                        ld(w2[k0:k1, k0:k1], I["L0_gnn_wk2_w"].rearrange("k d -> d k"))
                        ld(w2[k1:k2, k1:k2], I["L0_gnn_wv2_w"].rearrange("k d -> d k"))
                        ld(b2[:, k0:k1], I["L0_gnn_wk2_b"].unsqueeze(0))
                        ld(b2[:, k1:k2], I["L0_gnn_wv2_b"].unsqueeze(0))
                    for t, src in ((nat[0], "L0_gnn_out_w"), (nat[1], "L2_gnn_W1"), (nat[2], "L2_gnn_W2"),
                                   (w_p, "L1_gnn_Wp"), (w_g[0], "L1_gnn_W0"), (w_g[1], "L1_gnn_W1"),
                                   (w_g[2], "L1_gnn_W2"), (w_self, "L3_gnn_w_self")):
                        ld(t[:, :], I[src])
                    ld(wbas[:, :, :], I["L3_gnn_weight"].rearrange("b i o -> i b o"))
                    ld(alf[:, :, :].rearrange("p t b -> p (t b)"),
                       I["L3_gnn_alpha"].rearrange("t b -> (t b)").unsqueeze(0).to_broadcast([P, NT * NBAS]))
                n_loads.append(n[0])

            @block.tensor
            def _(pe):
                pe.wait_ge(s_ld.h, s_ld.at(16 * n_w))
                nc.tensor.matmul(pw[:, 0, 0:QW], qn[:, :], ql[:, :], start=True, stop=True).then_inc(s_t.h, 1)
                for k in range(3):
                    nc.tensor.transpose(pw[:, 1 + k, 0:D], nat[k][:, :], ident[:, :]).then_inc(s_t.h, 1)

            assert n_loads[-1] == n_w, n_loads
            s_x1.past(1)
            s_t.past(4)
            s_ld.past(16 * n_w)

        def affine(dve, link, t, k_mul, k_add):
            if k_mul is not None:
                link(dve.tensor_tensor(t[:, :, :], t[:, :, :], bc_mid(rowb[:, k_mul, :], NB), ALU.mult))
            link(dve.tensor_tensor(t[:, :, :], t[:, :, :], bc_mid(rowb[:, k_add, :], NB), ALU.add))

        def pre0(dve, link):
            link(dve.tensor_copy(V[:, :, :], X[:, :, :]))
            ln_dve(dve, link, s_rq, s_sd, V, Y)
            affine(dve, link, Y, 0, 1)

        dve_stage(pre0, rows=(I["L0_gnn_ln1_g"], I["L0_gnn_ln1_b"]), n_ln=1)
        node_mm(Y, [(w_kv[:, :], nodes(kv_t), ACT.Copy, True), (w_q[:, :], nodes(q_t), ACT.Copy, True)])

        def carve(big, *shapes):
            flat_, at_, out_ = big[:, :, :].rearrange("p b d -> p (b d)"), 0, []
            for sh in shapes:
                n = int(np.prod(sh))
                v = flat_[:, at_:at_ + n]
                if len(sh) == 2:
                    v = v.rearrange("p (a b) -> p a b", a=sh[0])
                if len(sh) == 3:
                    v = v.rearrange("p (a b c) -> p a b c", a=sh[0], b=sh[1])
                out_.append(v)
                at_ += n
            return out_

        qkA, ringU, ringR = carve(Y, (TS, NH), (2, HALF, D), (2, HALF, D))
        u_moved = [sem(f"products{h}_moved") for h in range(2)]
        s_aT = ring["attr_transposed"]
        s_aTc = ring["attr_copied"]
        s_hid = ring["hidden_sums"]
        s_rel = ring["relu_ready"]
        s_lg = ring["log_ready"]
        s_hr = ring["hidden_ready"]
        s_W = ring["edge_weights_ready"]
        s_u = ring["products_made"]
        s_lookq = ring["queries_ready"]
        s_ex = ring["exponentials_ready"]
        s_row = ring["message_rows_ready"]

        def half_steps(eng, body):
            with eng.Fori(0, ITM - 1) as i:
                for h in range(2):
                    body(i, h, lambda k: True)
            for h in range(2):
                body(ITM - 1, h, lambda k: h + k < 2)

        with ExitStack() as c:
            gk = sb(c, "gk", [P, 2, HALF], I32)
            KV, Qw, at = carve(Z, (2, HALF, 2 * D), (2, HALF, QW), (2, HALF, EC))
            U, t1, t2, ohT = carve(V, (2, HALF, D), (HALF, D), (HALF, D), (2, HALF, P))
            ohb = sb(c, "ohb", [P, 2, HALF, P], BF16)
            identb = sb(c, "identb", [P, P], BF16)
            aT = sb(c, "aT", [2 * EC, 2, HALF // 2 * P])
            sa, se, sl, sr, hid = [sb(c, n, [4 * KH, HALF // 2 * P]) for n in ("sa", "se", "sl", "sr", "hid")]
            pA, pH = ps(c, "pA", [2 * EC, 4, P]), ps(c, "pH", [4 * KH, 512])
            pW = ps(c, "pW", [P, 8, 2 * KH])
            pOT = ps(c, "pOT", [P, 8, P], BF16)
            pQ = ps(c, "pQ", [P, 2, HALF, 256])
            block = c.enter_context(nc.Block())

            @block.sync
            def _(sp):
                def load(j, h):
                    m, c0 = j * 2 + h, j * SLOTS + h * HALF
                    sp.wait_ge(s_aT.h, s_aT.at(m - 1))
                    sp.dma_start(at[:, h, :, :],
                                 rec_s.rearrange("(t p) f -> p t f", p=P)[:, bass.ds(c0, HALF), 4:RW])\
                        .then_inc(slot_landed[h].h, 16)
                    _, keys = nc.values_load_multi_w_load_instructions(
                        firstS[0:1, bass.ds(c0, HALF)], engines=(mybir.EngineType.SP,), min_val=0, max_val=N)
                    sp.wait_ge(s_lookq.h, s_lookq.at(m - 1))
                    for u, k in enumerate(keys):
                        sp.dma_start(Qw[:, h, u, :], q_t[bass.ds(k, P), :]).then_inc(g2_landed[h * HALF + u].h, 16)

                def step(i, h, later):
                    if later(2):
                        load(i + 1, h)
                    sp.wait_ge(s_u.h, s_u.at(i * 2 + h + 1))
                    sp.dma_start(u_d[:, bass.ds((i * SLOTS + h * HALF) * D, HALF * D)],
                                 U[:, h, :, :].rearrange("p u d -> p (u d)")).then_inc(u_moved[h].h, 16)

                load(0, 0)
                load(0, 1)
                half_steps(sp, step)
                for h in range(2):
                    sp.wait_ge(u_moved[h].h, u_moved[h].at(16 * ITM))

            @block.gpsimd
            def _(pool):
                set_bounds(pool, kv_t)
                with pool.Fori(0, ITM) as i:
                    for h in range(2):
                        pool.wait_ge(s_ix[h].h, s_ix[h].at(i + 1))
                        pool.wait_ge(s_u.h, s_u.at(i * 2 + h - 1))
                        carry()
                        for u in range(HALF):
                            gather(KV[:, h, u, :], kv_t, gk[:, h, u:u + 1], g_landed[h * HALF + u])

            @block.scalar
            def _(act):
                def indices(j, h):
                    for u in range(HALF):
                        act.wait_ge(g_landed[h * HALF + u].h, g_landed[h * HALF + u].at(16 * j))
                    nc.scalar.activation(gk[:, h, :], gdst_i[:, bass.ds(j * SLOTS + h * HALF, HALF)],
                                         ACT.Copy).then_inc(s_ix[h].h, 1)

                def copies(m, h):
                    act.wait_ge(s_ohT.h, s_ohT.at(m + 1))
                    act.wait_ge(s_lookq.h, s_lookq.at(m - 1))
                    nc.scalar.activation(ohT[:, h, :, :], pOT[:, 0:HALF, :], ACT.Copy).then_inc(s_ohc.h, 1)
                    act.wait_ge(s_aT.h, s_aT.at(m + 1))
                    act.wait_ge(s_hid.h, s_hid.at(m - 1))
                    nc.scalar.activation(aT[:, h, :], pA[:, 0:HALF // 2, :].rearrange("p u q -> p (u q)"),
                                         ACT.Copy).then_inc(s_aTc.h, 1)

                def hidden(m):
                    act.wait_ge(s_hid.h, s_hid.at(m + 1))
                    nc.scalar.activation(sa[:, :], pH[:, 0:HALF // 2 * P], ACT.Abs, bias=b1[:, 0:1]).then_inc(s_a.h, 1)
                    act.wait_ge(s_hr.h, s_hr.at(m))
                    nc.scalar.activation(sr[:, :], pH[:, 0:HALF // 2 * P], ACT.Relu,
                                         bias=b1[:, 0:1]).then_inc(s_rel.h, 1)
                    act.wait_ge(s_a.h, s_a.at(m * 2 + 1))
                    act.wait_ge(s_lg.h, s_lg.at(m))
                    nc.scalar.activation(se[:, :], sa[:, :], ACT.Exp, scale=-1.0).then_inc(s_a.h, 1)
                    act.wait_ge(s_a.h, s_a.at(m * 2 + 2))
                    nc.scalar.activation(sl[:, :], se[:, :], ACT.Ln, scale=0.5, bias=halfc[:, 0:1]).then_inc(s_lg.h, 1)

                def step(i, h, later):
                    if later(1):
                        hidden(i * 2 + h + 1)
                    if later(2):
                        copies(i * 2 + h + 2, h)
                        indices(i + 1, h)

                act.preload_act_table_set("natural_log_exp_and_others")
                indices(0, 0)
                indices(0, 1)
                copies(0, 0)
                hidden(0)
                copies(1, 1)
                half_steps(act, step)

            @block.tensor
            def _(pe):
                def transposes(m, j, h):
                    pe.wait_ge(slot_landed[h].h, slot_landed[h].at(j * 16 + 16))
                    pe.wait_ge(s_aTc.h, s_aTc.at(m))
                    for g in range(HALF // 2):
                        ins = nc.tensor.transpose(pA[:, g, :],
                                                  at[:, h, 2 * g:2 * g + 2, :].rearrange("p u d -> p (u d)"),
                                                  ident[:, :])
                    ins.then_inc(s_aT.h, 1)
                    pe.wait_ge(s_oh.h, s_oh.at(m + 1))
                    pe.wait_ge(s_ohc.h, s_ohc.at(m))
                    for u in range(HALF):
                        ins = nc.tensor.transpose(pOT[:, u, :], ohb[:, h, u, :], identb[:, :])
                    ins.then_inc(s_ohT.h, 1)

                def hidden(m, h):
                    pe.wait_ge(s_aTc.h, s_aTc.at(m + 1))
                    pe.wait_ge(s_a.h, s_a.at(m * 2))
                    pe.wait_ge(s_rel.h, s_rel.at(m))
                    nc.tensor.matmul(pH[:, 0:HALF // 2 * P], w1[:, :], aT[:, h, :], start=True,
                                     stop=True).then_inc(s_hid.h, 1)

                def queries(m, j, h):
                    pe.wait_ge(s_ohc.h, s_ohc.at(m + 1))
                    pe.wait_ge(s_u.h, s_u.at(m - 1))
                    for u in range(HALF):
                        pe.wait_ge(g2_landed[h * HALF + u].h, g2_landed[h * HALF + u].at(16 * j + 16))
                        ins = nc.tensor.matmul(pQ[:, h, u, 0:QW], ohT[:, h, u, :], Qw[:, h, u, :], start=True,
                                               stop=True)
                    ins.then_inc(s_lookq.h, 1)

                def step(i, h, later):
                    n = i * 2 + h
                    if later(1):
                        hidden(n + 1, 1 - h)
                    pe.wait_ge(s_hr.h, s_hr.at(n + 1))
                    pe.wait_ge(s_u.h, s_u.at(n))
                    for g in range(HALF // 2):
                        o = pW[:, 2 * g:2 * g + 2, :].rearrange("p u k -> p (u k)")
                        nc.tensor.matmul(o, hid[:, g * P:(g + 1) * P], w2[:, :], start=True, stop=False)
                        ins = nc.tensor.matmul(o, ones[0:1, :], b2[:, :], start=False, stop=True)
                    ins.then_inc(s_W.h, 1)
                    if later(1):
                        queries(n + 1, i + h, 1 - h)
                    if later(2):
                        transposes(n + 2, i + 1, h)

                transposes(0, 0, 0)
                hidden(0, 0)
                queries(0, 0, 0)
                transposes(1, 0, 1)
                half_steps(pe, step)

            @block.vector
            def _(dve):
                link0 = linker(dve, s_v)
                link0(dve.tensor_copy(identb[:, :], ident[:, :]))
                dve.memset(qkA[:, ITM * SLOTS:TS, :], 0.0)

                def onehots(m, h, c0):
                    dve.wait_ge(s_ohT.h, s_ohT.at(m - 1))
                    dve.tensor_tensor(ohb[:, h, :, :], bc_mid(ioh[:, :], HALF),
                                      bc_last(locS[:, bass.ds(c0, HALF)], P), ALU.is_equal).then_inc(s_oh.h, 1)

                def hidden(m):
                    dve.wait_ge(s_lg.h, s_lg.at(m + 1))
                    dve.wait_ge(s_rel.h, s_rel.at(m + 1))
                    dve.wait_ge(s_W.h, s_W.at(m))
                    dve.tensor_tensor(hid[:, :], sr[:, :], sl[:, :], ALU.add).then_inc(s_hr.h, 1)

                def step(i, h, later):
                    n, c0 = i * 2 + h, i * SLOTS + h * HALF

                    def link(ins, j):
                        ins.then_inc(s_v.h, 1)
                        dve.wait_ge(s_v.h, s_v.at(n * 4 + j))

                    def by_head(v):
                        return v.rearrange("p u (h k) -> p u h k", h=NH)

                    def each_head(w):
                        return w.unsqueeze(2).to_broadcast([P, HALF, NH, KH])

                    if later(2):
                        onehots(n + 2, h, c0 + SLOTS)
                    for u in range(HALF):
                        dve.wait_ge(g_landed[h * HALF + u].h, g_landed[h * HALF + u].at(16 * i + 16))
                    dve.wait_ge(s_lookq.h, s_lookq.at(n + 1))
                    link(dve.tensor_tensor(t1[:, :, :], KV[:, h, :, 0:D], pQ[:, h, :, 0:D], ALU.mult), 1)
                    dve.wait_ge(s_W.h, s_W.at(n + 1))
                    link(dve.tensor_tensor(by_head(t2[:, :, :]), by_head(t1[:, :, :]), each_head(pW[:, 0:HALF, 0:KH]),
                                           ALU.mult), 2)
                    scores = qkA[:, bass.ds(c0, HALF), :]
                    link(dve.tensor_reduce(scores, by_head(t2[:, :, :]), AX, ALU.add), 3)
                    link(dve.tensor_tensor(scores, scores, pQ[:, h, :, D:QW], ALU.add), 4)
                    dve.wait_ge(u_moved[h].h, u_moved[h].at(16 * i))
                    dve.tensor_tensor(by_head(U[:, h, :, :]), by_head(KV[:, h, :, D:2 * D]),
                                      each_head(pW[:, 0:HALF, KH:2 * KH]), ALU.mult).then_inc(s_u.h, 1)
                    if later(1):
                        hidden(n + 1)

                onehots(0, 0, 0)
                onehots(1, 1, HALF)
                hidden(0)
                half_steps(dve, step)

            for s in (s_aT, s_aTc, s_hid, s_lg, s_rel, s_hr, s_W, s_u, s_oh, s_ohT, s_ohc, s_lookq):
                s.past(2 * ITM)
            s_a.past(4 * ITM)
            s_v.past(8 * ITM)
            for h in range(2):
                s_ix[h].past(ITM)
                slot_landed[h].past(16 * ITM)
                u_moved[h].past(16 * ITM)
            for s in range(SLOTS):
                g_landed[s].past(16 * ITM)
                g2_landed[s].past(16 * ITM)

        NBK = TS // P
        with ExitStack() as c:
            (F,), (B,) = carve(Z, (NBK, NH * P)), carve(V, (NBK, NH * P))
            F = F.rearrange("t k (h p) -> t k h p", h=NH)
            B = B.rearrange("t k (h p) -> t k h p", h=NH)
            tmp = sb(c, "tmp", [P, NBK, NH, P])
            mk = sb(c, "mk", [P, NBK, P])
            S = sb(c, "S", [P, NBK, NH])
            K4 = sb(c, "K4", [P, NBK, NH])
            G = sb(c, "G", [NH, TS])
            KF, KL = sb(c, "KF", [NH, TS]), sb(c, "KL", [NH, TS])
            C = sb(c, "C", [NH, TS])
            g1, g2 = sb(c, "g1", [NH, TS]), sb(c, "g2", [NH, TS])
            CT = sb(c, "CT", [P, NBK, NH])
            pS = ps(c, "pS", [P, 2, HALF, P])
            pR = ps(c, "pR", [P, 2, 512])
            block = c.enter_context(nc.Block())

            def across(pe, src, n):
                pe.wait_ge(s_x1.h, s_x1.at(n))
                for k in range(NBK):
                    ins = nc.tensor.transpose(pR[0:NH, k // 4, (k % 4) * P:(k % 4 + 1) * P], src[:, k, :],
                                              ident[:, :])
                ins.then_inc(s_x2.h, 1)

            def back(pe, n):
                pe.wait_ge(s_x1.h, s_x1.at(n))
                for k in range(NBK):
                    ins = nc.tensor.transpose(pR[:, 0, k * NH:(k + 1) * NH], C[:, k * P:(k + 1) * P],
                                              ident[0:NH, 0:NH])
                ins.then_inc(s_x2.h, 1)

            @block.tensor
            def _(pe):
                pe.wait_ge(s_x3.h, s_x3.at(1))
                for k in range(NBK):
                    if k >= 2:
                        pe.wait_ge(s_x3.h, s_x3.at(k))
                    for h in range(NH):
                        ins = nc.tensor.transpose(pS[:, k % 2, h, :], qkA[:, k * P:(k + 1) * P, h], ident[:, :])
                    ins.then_inc(s_t.h, 1)
                across(pe, K4, 1)
                across(pe, K4, 2)
                across(pe, S, 3)
                back(pe, 4)
                across(pe, S, 5)
                back(pe, 6)
                for k in range(NBK):
                    pe.wait_ge(s_x4.h, s_x4.at(max(1, k)))
                    for h in range(NH):
                        ins = nc.tensor.transpose(pS[:, k % 2, h, :], F[:, k, h, :], ident[:, :])
                    ins.then_inc(s_t.h, 1)

            @block.vector
            def _(dve):
                link = linker(dve, s_v)
                r4 = bc_last(realS[:, :], NH)
                t4 = tmp[:, :, :, :].rearrange("t k h p -> t (k h p)").rearrange("p (t h) -> p t h", h=NH)
                link(dve.tensor_tensor(qkA[:, :, :], qkA[:, :, :], r4, ALU.mult))
                link(dve.tensor_scalar(t4, r4, -1.0, BIG, ALU.add, ALU.mult))
                dve.tensor_tensor(qkA[:, :, :], qkA[:, :, :], t4, ALU.add).then_inc(s_x3.h, 1)
                for k in range(NBK):
                    dve.wait_ge(s_t.h, s_t.at(k + 1))
                    dve.tensor_copy(F[:, k, :, :], pS[:, k % 2, :, :]).then_inc(s_x3.h, 1)
                dve.wait_ge(s_x3.h, s_x3.at(NBK + 1))
                link(dve.tensor_copy(B[:, :, :, :], F[:, :, :, :]))
                s = 1
                while s < P:
                    m = mk[:, :, 0:P - s]
                    link(dve.tensor_tensor(m, keyT[:, :, s:P], keyT[:, :, 0:P - s], ALU.not_equal))
                    link(dve.tensor_scalar(m, m, -BIG, None, ALU.mult))
                    for a, to, of in ((F, slice(s, P), slice(0, P - s)), (B, slice(0, P - s), slice(s, P))):
                        for k in range(NBK):
                            ins = dve.tensor_tensor(tmp[:, k, :, 0:P - s], a[:, k, :, of], bc_mid(mk[:, k, 0:P - s], NH),
                                                    ALU.add)
                        link(ins)
                        link(dve.tensor_tensor(a[:, :, :, to], a[:, :, :, to], tmp[:, :, :, 0:P - s], ALU.max))
                    s *= 2
                rowv = [pR[0:NH, 0, 0:512], pR[0:NH, 1, 0:TS - 512]]

                def from_rows(dst, n):
                    dve.wait_ge(s_x2.h, s_x2.at(n))
                    link(dve.tensor_copy(dst[:, 0:512], rowv[0]))
                    link(dve.tensor_copy(dst[:, 512:TS], rowv[1]))

                def signal():
                    dve.sem_inc(s_x1.h, 1)

                link(dve.tensor_copy(K4[:, :, :], keyT[:, :, 0:1].to_broadcast([P, NBK, NH])))
                signal()
                from_rows(KF, 1)
                link(dve.tensor_copy(K4[:, :, :], keyT[:, :, P - 1:P].to_broadcast([P, NBK, NH])))
                signal()
                from_rows(KL, 2)
                n = 3
                for a, edge, key, left in ((F, P - 1, KL, True), (B, 0, KF, False)):
                    link(dve.tensor_copy(S[:, :, :], a[:, :, :, edge]))
                    signal()
                    from_rows(G, n)
                    s = 1
                    while s < TS:
                        lo, hi = slice(0, TS - s), slice(s, TS)
                        to, of = (hi, lo) if left else (lo, hi)
                        link(dve.tensor_tensor(g1[:, 0:TS - s], key[:, hi], key[:, lo], ALU.not_equal))
                        link(dve.scalar_tensor_tensor(g2[:, 0:TS - s], g1[:, 0:TS - s], -BIG, G[:, of], ALU.mult,
                                                      ALU.add))
                        link(dve.tensor_tensor(G[:, to], G[:, to], g2[:, 0:TS - s], ALU.max))
                        s *= 2
                    to, of = (slice(1, TS), slice(0, TS - 1)) if left else (slice(0, TS - 1), slice(1, TS))
                    link(dve.memset(C[:, :], -BIG))
                    link(dve.tensor_tensor(g1[:, 0:TS - 1], KF[:, 1:TS], KL[:, 0:TS - 1], ALU.not_equal))
                    link(dve.scalar_tensor_tensor(C[:, to], g1[:, 0:TS - 1], -BIG, G[:, of], ALU.mult, ALU.add))
                    signal()
                    dve.wait_ge(s_x2.h, s_x2.at(n + 1))
                    link(dve.tensor_copy(CT[:, :, :], pR[:, 0, 0:NBK * NH].rearrange("p (k h) -> p k h", h=NH)))
                    for k in range(NBK):
                        e = 0 if left else P - 1
                        link(dve.tensor_scalar(mk[:, k, :], keyT[:, k, :], keyT[:, k, e:e + 1], -BIG, ALU.not_equal,
                                               ALU.mult))
                        for h in range(NH):
                            ins = dve.tensor_scalar(tmp[:, k, h, :], mk[:, k, :], CT[:, k, h:h + 1], None, ALU.add)
                        link(ins)
                    link(dve.tensor_tensor(a[:, :, :, :], a[:, :, :, :], tmp[:, :, :, :], ALU.max))
                    n += 2
                dve.tensor_tensor(F[:, :, :, :], F[:, :, :, :], B[:, :, :, :], ALU.max).then_inc(s_x4.h, 1)
                for k in range(NBK):
                    dve.wait_ge(s_t.h, s_t.at(NBK + k + 1))
                    v = qkA[:, k * P:(k + 1) * P, :]
                    dve.tensor_tensor(v, v, pS[:, k % 2, :, :].rearrange("p h t -> p t h"), ALU.subtract)\
                        .then_inc(s_x4.h, 1)

            @block.scalar
            def _(act):
                act.wait_ge(s_x4.h, s_x4.at(NBK + 1))
                nc.scalar.activation(qkA[:, :, :], qkA[:, :, :], ACT.Exp).then_inc(s_a.h, 1)

            @block.gpsimd
            def _(pool):
                pool.wait_ge(s_a.h, s_a.at(1))
                nc.gpsimd.tensor_tensor(qkA[:, :, :], qkA[:, :, :], bc_last(realS[:, :], NH), ALU.mult)

            s_x1.past(6)
            s_x2.past(6)
            s_x3.past(NBK + 1)
            s_x4.past(NBK + 1)
            s_t.past(2 * NBK)
            s_a.past(1)

        with ExitStack() as c:
            ex = sb(c, "ex", [P, 2, HALF, NH])
            oh = sb(c, "oh", [P, 2, HALF, P])
            resT = V[:, :, :].rearrange("p b d -> p (b d)")
            denT = Z[0:NH, :, :].rearrange("p b d -> p (b d)")
            pw, pd = ps(c, "pw", [P, 2, HALF, P]), ps(c, "pd", [P, 2, HALF, P])
            with nc.Block() as block:
                @block.sync
                def _(sp):
                    with sp.Fori(0, ITM) as i:
                        for h in range(2):
                            sp.wait_ge(s_row.h, s_row.at(i * 2 + h - 1))
                            sp.dma_start(ringU[:, h, :, :].rearrange("p u d -> p (u d)"),
                                         u_d[:, bass.ds((i * SLOTS + h * HALF) * D, HALF * D)])\
                                .then_inc(u_moved[h].h, 16)

                @block.gpsimd
                def _(pool):
                    with pool.Fori(0, ITM) as i:
                        for h in range(2):
                            n = i * 2 + h
                            pool.wait_ge(s_ex.h, s_ex.at(n + 1))
                            pool.wait_ge(u_moved[h].h, u_moved[h].at(16 * i + 16))
                            pool.wait_ge(s_cmb.h, s_cmb.at(n - 1))
                            nc.gpsimd.tensor_tensor(ringR[:, h, :, :].rearrange("p u (h k) -> p (u h) k", h=NH),
                                                    ringU[:, h, :, :].rearrange("p u (h k) -> p (u h) k", h=NH),
                                                    bc_last(ex[:, h, :, :].rearrange("p u h -> p (u h)"), KH),
                                                    ALU.mult).then_inc(s_row.h, 1)

                @block.scalar
                def _(act):
                    with act.Fori(0, ITM) as i:
                        for h in range(2):
                            c0 = i * SLOTS + h * HALF
                            act.wait_ge(s_cmb.h, s_cmb.at(i * 2 + h - 1))
                            nc.scalar.activation(ex[:, h, :, :], qkA[:, bass.ds(c0, HALF), :],
                                                 ACT.Copy).then_inc(s_ex.h, 1)

                @block.tensor
                def _(pe):
                    with pe.Fori(0, ITM) as i:
                        for h in range(2):
                            n = i * 2 + h
                            pe.wait_ge(s_eq.h, s_eq.at(n + 1))
                            pe.wait_ge(s_stg.h, s_stg.at((n - 1) * HALF))
                            pe.wait_ge(s_row.h, s_row.at(n + 1))
                            for u in range(HALF):
                                nc.tensor.matmul(pw[:, h, u, :], ringR[:, h, u, :], oh[:, h, u, :], start=True,
                                                 stop=True)
                                ins = nc.tensor.matmul(pd[0:NH, h, u, :], ex[:, h, u, :], oh[:, h, u, :], start=True,
                                                       stop=True)
                            ins.then_inc(s_cmb.h, 1)

                @block.vector
                def _(dve):
                    link = linker(dve, s_v)
                    link(dve.memset(resT, 0.0))
                    link(dve.memset(denT, 0.0))

                    def onehots(m, h, c0):
                        dve.wait_ge(s_cmb.h, s_cmb.at(m - 1))
                        dve.tensor_tensor(oh[:, h, :, :], bc_mid(ioh[:, :], HALF),
                                          bc_last(locS[:, bass.ds(c0, HALF)], P), ALU.is_equal).then_inc(s_eq.h, 1)

                    def step(i, h, later):
                        n, c0 = i * 2 + h, i * SLOTS + h * HALF
                        _, keys = nc.values_load_multi_w_load_instructions(
                            firstS[0:1, bass.ds(c0, HALF)], engines=(mybir.EngineType.DVE,), min_val=0, max_val=N)
                        dve.wait_ge(s_cmb.h, s_cmb.at(n + 1))
                        for u, k in enumerate(keys):
                            dve.wait_ge(s_stg.h, s_stg.at(n * HALF + u))
                            a, b = resT[:, bass.ds(k, P)], denT[:, bass.ds(k, P)]
                            dve.tensor_tensor(b, b, pd[0:NH, h, u, :], ALU.add)
                            dve.tensor_tensor(a, a, pw[:, h, u, :], ALU.add).then_inc(s_stg.h, 1)
                        if later(2):
                            onehots(n + 2, h, c0 + SLOTS)

                    onehots(0, 0, 0)
                    onehots(1, 1, HALF)
                    half_steps(dve, step)

                for s in (s_eq, s_cmb, s_ex, s_row):
                    s.past(2 * ITM)
                s_stg.past(2 * ITM * HALF)
                for h in range(2):
                    u_moved[h].past(16 * ITM)
            turn_back(c, resT, Y)

        den = sb(top, "den", [P, NB, NH])
        with ExitStack() as c:
            turn_back(c, Z[0:NH, :, :].rearrange("p b d -> p (b d)"), den)
        dt0, dt1 = sb(top, "dt0", [P, NB, NH]), sb(top, "dt1", [P, NB, NH])

        def heads(t):
            return t[:, :, :].rearrange("p b (h k) -> p (b h) k", h=NH)

        def flat(t):
            return t[:, :, :].rearrange("p b h -> p (b h)")

        def norm0(dve, link):
            link(dve.tensor_scalar(flat(dt0), flat(den), 1e-30, None, ALU.max))
            link(dve.reciprocal(flat(dt0), flat(dt0)))
            link(dve.tensor_tensor(flat(dt1), flat(den), flat(dt0), ALU.mult))
            link(dve.tensor_tensor(heads(Y), heads(Y), bc_last(flat(dt0), KH), ALU.mult))

        dve_stage(norm0)
        node_mm(Y, [(w_vl[:, :], Z, ACT.Copy, False)])

        def mid0(dve, link):
            for h in range(NH):
                link(dve.tensor_tensor(V[:, :, h * KH:(h + 1) * KH], bc_mid(rowb[:, 2, 0:KH], NB),
                                       bc_last(dt1[:, :, h], KH), ALU.mult))
            link(dve.tensor_tensor(Z[:, :, :], Z[:, :, :], V[:, :, :], ALU.add))
            link(dve.tensor_tensor(Z[:, :, :], Z[:, :, :], X[:, :, :], ALU.add))
            link(dve.tensor_copy(V[:, :, :], Z[:, :, :]))
            ln_dve(dve, link, s_rq, s_sd, V, Y)
            affine(dve, link, Y, 0, 1)

        dve_stage(mid0, rows=(I["L0_gnn_ln2_g"], I["L0_gnn_ln2_b"], I["L0_gnn_wvl_b"]), n_ln=1)

        def act_stage(body):
            with ExitStack() as c:
                block = c.enter_context(nc.Block())

                @block.scalar
                def _(act):
                    body(act, linker(act, s_a))

        def ssp0(act, link):
            link(nc.scalar.activation(V[:, :, :], Y[:, :, :], ACT.Abs))
            link(nc.scalar.activation(V[:, :, :], V[:, :, :], ACT.Exp, scale=-1.0))
            link(nc.scalar.activation(V[:, :, :], V[:, :, :], ACT.Ln, scale=0.5, bias=halfc[:, 0:1]))

        act_stage(ssp0)

        def hid0(dve, link):
            link(dve.scalar_tensor_tensor(Y[:, :, :], Y[:, :, :], 0.0, V[:, :, :], ALU.max, ALU.add))

        dve_stage(hid0)
        node_mm(Y, [(w_out[:, :], V, ACT.Copy, False)])

        def post0(dve, link):
            affine(dve, link, V, None, 0)
            link(dve.tensor_tensor(V[:, :, :], V[:, :, :], Z[:, :, :], ALU.add))
            link(dve.tensor_tensor(V[:, :, :], V[:, :, :], X[:, :, :], ALU.add))
            ln_dve(dve, link, s_rq, s_sd, V, X)

        dve_stage(post0, rows=(I["L0_gnn_out_b"],), n_ln=1)

        node_mm(X, [(w_p[:, :], Y, ACT.Copy, False)])

        def deg1(dve, link):
            affine(dve, link, Y, None, 0)
            dve.tensor_scalar(red[:, :], degd[:, :], 1e-30, None, ALU.max).then_inc(s_rq.h, 1)
            s_rq.past(1)
            s_sd.past(1)
            dve.wait_ge(s_sd.h, s_sd.base)
            link(dve.reciprocal(dinv[:, :], red2[:, :]))

        dve_stage(deg1, rows=(I["L1_gnn_bp"],), n_ln=1)
        act_stage(lambda act, link: link(nc.scalar.activation(Y[:, :, :], Y[:, :, :], ACT.Gelu)))
        for k in range(3):
            node_mm(Y, [(w_g[k][:, :], Z, ACT.Copy, False)])
            dve_stage(lambda dve, link: link(dve.tensor_tensor(Z[:, :, :], Z[:, :, :], bc_last(dinv[:, :], D),
                                                               ALU.mult)))
            load_store([(nodes(h_t), Z[:, :, :])])
            window_sum(h_t, gsrc_i, None, locD, firstD, Y)

            def conv(dve, link):
                link(dve.tensor_tensor(Y[:, :, :], Y[:, :, :], bc_last(dinv[:, :], D), ALU.mult))
                affine(dve, link, Y, None, 0)

            dve_stage(conv, rows=(I[f"L1_gnn_b{k}"],))

        def post1(dve, link):
            link(dve.tensor_tensor(Y[:, :, :], Y[:, :, :], X[:, :, :], ALU.add))
            ln_dve(dve, link, s_rq, s_sd, Y, X)

        dve_stage(post1, n_ln=1)

        load_store([(nodes(h_t), X[:, :, :])])
        window_sum(h_t, gsrc_i, wD, locD, firstD, Y)

        def pre2(dve, link):
            link(dve.tensor_tensor(Z[:, :, :], Y[:, :, :], X[:, :, :], ALU.mult))
            link(dve.tensor_tensor(Y[:, :, :], Y[:, :, :], X[:, :, :], ALU.add))

        dve_stage(pre2)
        node_mm(Y, [(w_n1[:, :], V, ACT.Copy, False)])
        node_mm(Z, [(w_n2[:, :], Y, ACT.Copy, False)])

        def post2(dve, link):
            link(dve.tensor_tensor(V[:, :, :], V[:, :, :], Y[:, :, :], ALU.add))
            affine(dve, link, V, None, 0)
            affine(dve, link, V, None, 1)
            link(dve.scalar_tensor_tensor(V[:, :, :], V[:, :, :], 0.2, V[:, :, :], ALU.mult, ALU.max))
            link(dve.tensor_tensor(V[:, :, :], V[:, :, :], X[:, :, :], ALU.add))
            ln_dve(dve, link, s_rq, s_sd, V, X)

        dve_stage(post2, rows=(I["L2_gnn_b1"], I["L2_gnn_b2"]), n_ln=1)

        rel_v = rel_t.rearrange("(p b t) d -> p b (t d)", b=NB, t=NT)
        node_mm(X, [(w_rel[:, k * 512:(k + 1) * 512], rel_v[:, :, k * 512:(k + 1) * 512], ACT.Copy, True)
                    for k in range(NT * D // 512)])
        window_sum(rel_t, grel_i, wS, locS, firstS, Y)
        node_mm(X, [(w_self[:, :], V, ACT.Copy, False)])

        def post3(dve, link):
            link(dve.tensor_scalar(degs[:, :], degs[:, :], 1e-12, None, ALU.max))
            link(dve.reciprocal(degs[:, :], degs[:, :]))
            link(dve.tensor_tensor(Y[:, :, :], Y[:, :, :], bc_last(degs[:, :], D), ALU.mult))
            ln_dve(dve, link, s_rq, s_sd, Y, Z)
            affine(dve, link, Z, 0, 1)
            affine(dve, link, Z, None, 2)
            link(dve.tensor_tensor(Z[:, :, :], Z[:, :, :], V[:, :, :], ALU.add))
            link(dve.tensor_tensor(Z[:, :, :], Z[:, :, :], X[:, :, :], ALU.add))
            ln_dve(dve, link, s_rq, s_sd, Z, Y)

        dve_stage(post3, rows=(I["L3_gnn_ln_gamma"], I["L3_gnn_ln_beta"], I["L3_gnn_bias"]), n_ln=2)
        load_store([(out.rearrange("(p b) d -> p b d", b=NB), Y[0:PU, :, :])])
    return nc


_INS = ["x", "src", "dst", "edge_attr_64", "edge_type_16", "edge_weight", "L0_gnn_k_w", "L0_gnn_q_w", "L0_gnn_v_w",
        "L0_gnn_wk1_w", "L0_gnn_wk1_b", "L0_gnn_wk2_w", "L0_gnn_wk2_b", "L0_gnn_wkl_w", "L0_gnn_wkl_b",
        "L0_gnn_wv1_w", "L0_gnn_wv1_b", "L0_gnn_wv2_w", "L0_gnn_wv2_b", "L0_gnn_wvl_w", "L0_gnn_wvl_b",
        "L0_gnn_out_w", "L0_gnn_out_b", "L0_gnn_ln1_g", "L0_gnn_ln1_b", "L0_gnn_ln2_g", "L0_gnn_ln2_b",
        "L1_gnn_Wp", "L1_gnn_bp", "L1_gnn_W0", "L1_gnn_b0", "L1_gnn_W1", "L1_gnn_b1", "L1_gnn_W2", "L1_gnn_b2",
        "L2_gnn_W1", "L2_gnn_b1", "L2_gnn_W2", "L2_gnn_b2", "L3_gnn_weight", "L3_gnn_alpha", "L3_gnn_bias",
        "L3_gnn_w_self", "L3_gnn_ln_gamma", "L3_gnn_ln_beta"]


def kernel(**inputs):
    import numpy as _np
    import concourse.bacc as _bacc
    from concourse import mybir as _mybir
    from concourse.bass_utils import run_bass_kernel_spmd as _run

    nc = _bacc.Bacc("TRN2", target_bir_lowering=False, num_devices=1)
    arrays, aps = {}, {}
    for name in _INS:
        a = _np.ascontiguousarray(inputs[name])
        arrays[f"in_{name}_dram"] = a
        aps[name] = nc.dram_tensor(f"in_{name}_dram", a.shape, _mybir.dt.from_np(a.dtype), kind="ExternalInput").ap()
    out = nc.dram_tensor("out_dram", inputs["x"].shape, _mybir.dt.float32, kind="ExternalOutput").ap()
    build(nc, aps, out)
    r = _run(nc, [arrays], core_ids=[0])
    return r.results[0]["out_dram"]
```
